# Optimizing a Trainium2 kernel written in Bass

```python
import numpy as np
import jax
import jax.numpy as jnp

def _softmax(x, axis=-1):
    return jax.nn.softmax(x, axis=axis)

def _gelu(x):
    return jax.nn.gelu(x, approximate=True)

def _silu(x):
    return jax.nn.silu(x)

def _sigmoid(x):
    return jax.nn.sigmoid(x)

def _layernorm(x, axis=-1, eps=1e-05):
    m = jnp.mean(x, axis=axis, keepdims=True)
    v = jnp.var(x, axis=axis, keepdims=True)
    return (x - m) / jnp.sqrt(v + eps)

def _scatter_add(tgt, idx, src, axis=0):
    return tgt.at[idx].add(src)

def _segment_sum(src, seg, n):
    return jax.ops.segment_sum(src, seg, n)
kernel_name = 'mk_adj_resnorm_d4_adj_r2_a528d3'

def setup_inputs(seed: int=0):
    np.random.seed(seed)
    _w = jnp.asarray

    def _rec_inputs():
        import jax
        import jax.numpy as jnp
        _gk = jax.random.key(seed)
        x = -0.000929 + 1 * jax.random.normal(jax.random.fold_in(_gk, 1), (4096, 128), jnp.float32)
        _a = jax.random.bernoulli(jax.random.fold_in(_gk, 2), 0.000488281, (4096, 4096))
        _a = jnp.logical_or(_a, jnp.eye(4096, dtype=bool))
        _af = _a.astype(jnp.float32)
        _af = _af * jax.random.uniform(jax.random.fold_in(_gk, 3), (4096, 4096), jnp.float32, 0.05, 1)
        adj = _af
        return (x, adj)
    x, adj = _rec_inputs()

    def _L0_gnn_setup():
        import jax, jax.numpy as jnp
        import numpy as np
        N = 4096
        H = 128
        key = jax.random.key(seed)
        k_x, k_A, k_W = jax.random.split(key, 3)
        x = jax.random.normal(k_x, (N, H), dtype=jnp.float32)
        A = jax.random.uniform(k_A, (N, N), dtype=jnp.float32)
        alpha = jnp.array([0.5], dtype=jnp.float32)
        bound = 1.0 / np.sqrt(H)
        W = jax.random.uniform(k_W, (H, H), dtype=jnp.float32, minval=-bound, maxval=bound)
        b = jnp.zeros((H,), dtype=jnp.float32)
        t = jnp.zeros((1,), dtype=jnp.float32)
        return {'t': t, 'x': x, 'A': A, 'alpha': alpha, 'W': W, 'b': b}
    _L0_gnn_all = _L0_gnn_setup()
    _L0_gnn_in = {k: v for k, v in _L0_gnn_all.items() if k in ('t', 'alpha', 'W', 'b')}
    del _L0_gnn_all

    def _L1_gnn_setup():
        import jax, jax.numpy as jnp
        import numpy as np
        N = 8192
        F_IN = 128
        F_OUT = 128
        key = jax.random.key(seed)
        k1, k2, k3, k4 = jax.random.split(key, 4)
        features = jax.random.normal(k1, (N, F_IN), dtype=jnp.float32)
        adj = jax.random.uniform(k2, (N, N), dtype=jnp.float32)
        kernel = jax.random.normal(k3, (F_IN, F_OUT), dtype=jnp.float32) * 0.02
        bias = jax.random.normal(k4, (F_OUT,), dtype=jnp.float32) * 0.02
        return {'features': features, 'adj': adj, 'kernel': kernel, 'bias': bias}
    _L1_gnn_all = _L1_gnn_setup()
    _L1_gnn_in = {k: v for k, v in _L1_gnn_all.items() if k in ('kernel', 'bias')}
    del _L1_gnn_all

    def _L2_gnn_setup():
        import jax, jax.numpy as jnp
        import numpy as np
        N, D = (4096, 128)
        EDGE_PROB = 0.005
        COS_EPS = 1e-08
        key = jax.random.key(seed)
        kx, ka = jax.random.split(key)
        x = jax.random.normal(kx, (N, D), dtype=jnp.float32)
        adj = (jax.random.uniform(ka, (N, N)) < EDGE_PROB).astype(jnp.float32)
        return {'t': jnp.float32(0.0), 'x': x, 'adj': adj, 'alpha': jnp.float32(0.5), 'beta': jnp.float32(1.0)}
    _L2_gnn_all = _L2_gnn_setup()
    _L2_gnn_in = {k: v for k, v in _L2_gnn_all.items() if k in ('t', 'alpha', 'beta')}
    del _L2_gnn_all

    def _L3_gnn_setup():
        import jax, jax.numpy as jnp
        import numpy as np
        N, IN, H, C = (2048, 128, 4, 32)
        HC = H * C
        EDGE_P = 0.008

        def _linear_params(key, fan_in, fan_out, bias=True):
            k1, k2 = jax.random.split(key)
            lim = 1.0 / np.sqrt(fan_in)
            W = jax.random.uniform(k1, (fan_in, fan_out), jnp.float32, -lim, lim)
            if not bias:
                return W
            b = jax.random.uniform(k2, (fan_out,), jnp.float32, -lim, lim)
            return (W, b)

        def _transformer_conv(x, adj, Wq, bq, Wk, bk, Wv, bv, Ws, bs, Wb):
            n = x.shape[0]
            q = (x @ Wq + bq).reshape(n, H, C)
            k = (x @ Wk + bk).reshape(n, H, C)
            v = (x @ Wv + bv).reshape(n, H, C)
            attn = jnp.einsum('nhc,mhc->hnm', q, k) / np.float32(np.sqrt(C))
            mask = adj == 0.0
            neg = jnp.where(mask[None], -jnp.inf, attn)
            m = jnp.max(neg, axis=-1, keepdims=True)
            all_inf = jnp.isneginf(m)
            e = jnp.where(mask[None], 0.0, jnp.exp(neg - jnp.where(all_inf, 0.0, m)))
            denom = jnp.sum(e, axis=-1, keepdims=True)
            alpha = e / jnp.where(denom == 0.0, 1.0, denom)
            out = jnp.einsum('hnm,mhc->hnc', alpha, v)
            out = jnp.transpose(out, (1, 2, 0)).reshape(n, C * H)
            x_r = x @ Ws + bs
            beta = jax.nn.sigmoid(jnp.concatenate([out, x_r, out - x_r], axis=-1) @ Wb)
            return beta * x_r + (1.0 - beta) * out
        key = jax.random.key(seed)
        ks = jax.random.split(key, 7)
        x = jax.random.normal(ks[0], (N, IN), jnp.float32)
        adj = (jax.random.uniform(ks[1], (N, N)) < EDGE_P).astype(jnp.float32)
        Wq, bq = _linear_params(ks[2], IN, HC)
        Wk, bk = _linear_params(ks[3], IN, HC)
        Wv, bv = _linear_params(ks[4], IN, HC)
        Ws, bs = _linear_params(ks[5], IN, HC)
        Wb = _linear_params(ks[6], 3 * HC, 1, bias=False)
        return dict(x=x, adj=adj, Wq=Wq, bq=bq, Wk=Wk, bk=bk, Wv=Wv, bv=bv, Ws=Ws, bs=bs, Wb=Wb)
    _L3_gnn_all = _L3_gnn_setup()
    _L3_gnn_in = {k: v for k, v in _L3_gnn_all.items() if k in ('Wq', 'bq', 'Wk', 'bk', 'Wv', 'bv', 'Ws', 'bs', 'Wb')}
    del _L3_gnn_all
    return {'x': x, 'adj': adj, 'L0_gnn_t': _L0_gnn_in['t'], 'L0_gnn_alpha': _L0_gnn_in['alpha'], 'L0_gnn_W': _L0_gnn_in['W'], 'L0_gnn_b': _L0_gnn_in['b'], 'L1_gnn_kernel': _L1_gnn_in['kernel'], 'L1_gnn_bias': _L1_gnn_in['bias'], 'L2_gnn_t': _L2_gnn_in['t'], 'L2_gnn_alpha': _L2_gnn_in['alpha'], 'L2_gnn_beta': _L2_gnn_in['beta'], 'L3_gnn_Wq': _L3_gnn_in['Wq'], 'L3_gnn_bq': _L3_gnn_in['bq'], 'L3_gnn_Wk': _L3_gnn_in['Wk'], 'L3_gnn_bk': _L3_gnn_in['bk'], 'L3_gnn_Wv': _L3_gnn_in['Wv'], 'L3_gnn_bv': _L3_gnn_in['bv'], 'L3_gnn_Ws': _L3_gnn_in['Ws'], 'L3_gnn_bs': _L3_gnn_in['bs'], 'L3_gnn_Wb': _L3_gnn_in['Wb']}

def reference(x, adj, L0_gnn_t, L0_gnn_alpha, L0_gnn_W, L0_gnn_b, L1_gnn_kernel, L1_gnn_bias, L2_gnn_t, L2_gnn_alpha, L2_gnn_beta, L3_gnn_Wq, L3_gnn_bq, L3_gnn_Wk, L3_gnn_bk, L3_gnn_Wv, L3_gnn_bv, L3_gnn_Ws, L3_gnn_bs, L3_gnn_Wb):
    import jax
    import jax.numpy as jnp

    def _L0_gnn_ref(t, x, A, alpha, W, b):
        import jax, jax.numpy as jnp
        import numpy as np
        N = 4096
        H = 128
        a = alpha[0]
        A_prime = a * A
        diag = jnp.diagonal(A_prime) + (1.0 - a)
        A_prime = A_prime.at[jnp.arange(N), jnp.arange(N)].set(diag)
        out_degree = A_prime.sum(axis=1)
        inv_deg = jnp.where(out_degree == 0.0, 0.0, 1.0 / out_degree)
        x = inv_deg[:, None] * A_prime @ x
        x = x @ W.T + b
        return jax.nn.relu(x)

    def _L1_gnn_ref(features, adj, kernel, bias):
        import jax, jax.numpy as jnp
        import numpy as np
        N = 8192
        F_IN = 128
        F_OUT = 128
        xw = features @ kernel
        out = adj @ xw
        return jax.nn.relu(out + bias)

    def _L2_gnn_ref(t, x, adj, alpha, beta):
        import jax, jax.numpy as jnp
        import numpy as np
        N, D = (4096, 128)
        EDGE_PROB = 0.005
        COS_EPS = 1e-08
        deg = jnp.clip(adj.sum(axis=1), 1.0)
        dis = deg ** (-0.5)
        adj_norm = dis[:, None] * adj * dis[None, :]
        diffusion = adj_norm @ x - x
        norms = jnp.maximum(jnp.linalg.norm(x, axis=-1), COS_EPS)
        sim = x @ x.T / (norms[:, None] * norms[None, :])
        attn = jax.nn.softmax(beta * sim * adj, axis=1)
        attn = jax.lax.stop_gradient(attn)
        return diffusion + jax.nn.sigmoid(alpha) * (attn @ x - x)

    def _L3_gnn_ref(x, adj, Wq, bq, Wk, bk, Wv, bv, Ws, bs, Wb):
        import jax, jax.numpy as jnp
        import numpy as np
        N, IN, H, C = (2048, 128, 4, 32)
        HC = H * C
        EDGE_P = 0.008

        def _linear_params(key, fan_in, fan_out, bias=True):
            k1, k2 = jax.random.split(key)
            lim = 1.0 / np.sqrt(fan_in)
            W = jax.random.uniform(k1, (fan_in, fan_out), jnp.float32, -lim, lim)
            if not bias:
                return W
            b = jax.random.uniform(k2, (fan_out,), jnp.float32, -lim, lim)
            return (W, b)

        def _transformer_conv(x, adj, Wq, bq, Wk, bk, Wv, bv, Ws, bs, Wb):
            n = x.shape[0]
            q = (x @ Wq + bq).reshape(n, H, C)
            k = (x @ Wk + bk).reshape(n, H, C)
            v = (x @ Wv + bv).reshape(n, H, C)
            attn = jnp.einsum('nhc,mhc->hnm', q, k) / np.float32(np.sqrt(C))
            mask = adj == 0.0
            neg = jnp.where(mask[None], -jnp.inf, attn)
            m = jnp.max(neg, axis=-1, keepdims=True)
            all_inf = jnp.isneginf(m)
            e = jnp.where(mask[None], 0.0, jnp.exp(neg - jnp.where(all_inf, 0.0, m)))
            denom = jnp.sum(e, axis=-1, keepdims=True)
            alpha = e / jnp.where(denom == 0.0, 1.0, denom)
            out = jnp.einsum('hnm,mhc->hnc', alpha, v)
            out = jnp.transpose(out, (1, 2, 0)).reshape(n, C * H)
            x_r = x @ Ws + bs
            beta = jax.nn.sigmoid(jnp.concatenate([out, x_r, out - x_r], axis=-1) @ Wb)
            return beta * x_r + (1.0 - beta) * out
        return _transformer_conv(x, adj, Wq, bq, Wk, bk, Wv, bv, Ws, bs, Wb)
    x = _layernorm(x + _L0_gnn_ref(L0_gnn_t, x, adj, L0_gnn_alpha, L0_gnn_W, L0_gnn_b), axis=-1)
    x = _layernorm(x + _L1_gnn_ref(x, adj, L1_gnn_kernel, L1_gnn_bias), axis=-1)
    x = _layernorm(x + _L2_gnn_ref(L2_gnn_t, x, adj, L2_gnn_alpha, L2_gnn_beta), axis=-1)
    x = _layernorm(x + _L3_gnn_ref(x, adj, L3_gnn_Wq, L3_gnn_bq, L3_gnn_Wk, L3_gnn_bk, L3_gnn_Wv, L3_gnn_bv, L3_gnn_Ws, L3_gnn_bs, L3_gnn_Wb), axis=-1)
    return x

_drawn_inputs = setup_inputs


def setup_inputs(seed=0):
    import zlib

    import numpy as np

    out = dict(_drawn_inputs(seed))
    spreads = {'L0_gnn_b': (0.0, 0.1)}
    factors = {'L3_gnn_bq': 8.0, 'L3_gnn_bk': 8.0}
    for name, (base, spread) in spreads.items():
        noise = np.random.default_rng([zlib.crc32(name.encode()), seed]).standard_normal(out[name].shape)
        drawn = base * np.exp(spread * noise) if base else spread * noise
        out[name] = jnp.asarray(drawn.astype(out[name].dtype))
    for name, factor in factors.items():
        out[name] = (out[name] * factor).astype(out[name].dtype)
    return out
```

```python
from contextlib import ExitStack

import concourse.bass as bass
from concourse import mybir

F32 = mybir.dt.float32
F32R = mybir.dt.float32r
BF16 = mybir.dt.bfloat16
ALU = mybir.AluOpType
ACT = mybir.ActivationFunctionType
AX = mybir.AxisListType

P = 128
N = 4096
D = 128
NT = N // P
CW = 512
NC = N // CW
CT = CW // P
GROUPS = 4
GT = NT // GROUPS
HW = 256
HC = N // HW
HT = HW // P
QW = 1024
NQ = N // QW
HEADS, C = 4, 32
EPS = 1e-5
MASKED = -1.0e30
FLOOR = -1.0e29


def wait(eng, sem, value):
    if isinstance(value, int) and value <= 0:
        return
    eng.wait_ge(sem, value)


def apart(eng, passed):
    eng.sem_inc(passed, 1)


class Chain:

    def __init__(self, eng, sem, per):
        self.eng, self.sem, self.per = eng, sem, per

    def round(self, j):
        self.base, self.k = self.per * j, 0

    def add(self, ins):
        ins.then_inc(self.sem, 1)
        self.k += 1

    def sync(self):
        self.eng.wait_ge(self.sem, self.base + self.k)

    def link(self, ins):
        self.add(ins)
        self.sync()

    def done(self):
        assert self.k == self.per, (self.k, self.per)


def lagged(eng, n, lag, body):
    for j in range(2):
        body(j, j)
    with eng.Fori(1, n // 2) as t:
        for b in range(2):
            body(2 * t + b, b)
    for j in range(n, n + lag):
        body(j, j % 2)


def inside(j, n):
    return not isinstance(j, int) or 0 <= j < n


def graph_layers(nc, a):
    ctx = ExitStack()
    with ctx:
        def sem(name):
            return ctx.enter_context(nc.semaphore(name))

        def sb(name, shape, dt=F32, at=ctx):
            return at.enter_context(nc.sbuf_tensor(name, shape, dt))

        def ps(name, shape):
            return ctx.enter_context(nc.psum_tensor(name, shape, F32))

        pair = [ps(f"pair{k}", [P, QW]) for k in range(2)]
        turned = [ps(f"turned{k}", [P, CW]) for k in range(3)]
        sums = ps("sums", [P, CW])
        banks = [pair[0][:, 0:CW], pair[0][:, CW:QW], pair[1][:, 0:CW], pair[1][:, CW:QW]]

        xa = sb("xa", [P, N])
        xb = sb("xb", [P, N])
        ident = sb("ident", [P, P])
        stack = sb("stack", [P, C])
        ones = sb("ones", [P, 1])
        w0 = sb("w0", [D, D])
        w1 = sb("w1", [D, D])
        bias0 = sb("bias0", [P, D])
        bias1 = sb("bias1", [P, D])
        wq = sb("wq", [D, D])
        wk = sb("wk", [D, HEADS, 4, C])
        bq = sb("bq", [P, 1])
        bk = sb("bk", [P, HEADS])
        wv = sb("wv", [D, D])
        ws = sb("ws", [D, D])
        bias_v = sb("bias_v", [P, D])
        bias_s = sb("bias_s", [P, D])
        gate_w = sb("gate_w", [P, 3 * D])
        gate_out = sb("gate_out", [P, D])
        gate_skip = sb("gate_skip", [P, D])
        scal = sb("scal", [P, 8])
        alpha0, alpha2, beta2 = scal[:, 0:1], scal[:, 1:2], scal[:, 2:3]
        keep0, sig_e, sig_d, sig2, negsig2 = (scal[:, k:k + 1] for k in range(3, 8))
        half = sb("half", [P, 1])
        rowsum = sb("rowsum", [P, NT])
        dis_t = sb("dis_t", [P, NT])
        dis = sb("dis", [P, NT])
        stats = sb("stats", [P, CT, 6])
        mv = sb("mv", [P, CT, 2])
        var_e = sb("var_e", [P, CT])
        rstd = sb("rstd", [P, CT])
        skip_dram = nc.dram_tensor("skip_dram", (HC, P, HT, D), F32, kind="Internal").ap()
        q_dram = nc.dram_tensor("q_dram", (2, HEADS * C, N), F32, kind="Internal").ap()

        l12 = ExitStack()
        xn_hi = sb("xn_hi", [D, N], F32R, l12)
        xn_lo = sb("xn_lo", [D, N], F32R, l12)
        l01 = ExitStack()
        cols = [sb(f"cols{g}", [P, 2, GT, HW], F32, l01) for g in range(GROUPS)]
        keep_xt = sb("keep_xt", [D, N], F32, l01)
        part = [sb(f"part{b}", [P, GROUPS, CW], F32, l01) for b in range(2)]
        agg = [sb(f"agg{b}", [D, CW], F32, l01) for b in range(2)]
        lin = sb("lin", [P, CW], F32, l01)
        res = sb("res", [P, CW], F32, l01)
        xn = sb("xn", [P, CW], F32, l01)
        sq = sb("sq", [P, CW], F32, l01)
        small = sb("small", [P, 6, CT], F32, l01)
        deg, deg_safe, deg_nz, deg_inv, inv = (small[:, k, :] for k in range(5))
        ssq = sb("ssq", [P, 3, CT], F32, l01)
        l01.close()
        l2 = ExitStack()
        rows2 = [sb(f"rows2_{i}", [P, N], F32, l2) for i in range(HT)]
        cols2 = [sb(f"cols2_{k}", [P, 4, HW], F32, l2) for k in range(4)]
        prob = [[sb(f"prob{b}{i}", [P, N], F32, l2) for i in range(HT)] for b in range(2)]
        mix = [sb(f"mix{k}", [P, 2, HW], F32, l2) for k in range(4)]
        st_hi = [sb(f"st_hi{b}", [D, HW], F32R, l2) for b in range(2)]
        st_lo = [sb(f"st_lo{b}", [D, HW], F32R, l2) for b in range(2)]
        agg2 = sb("agg2", [D, HW], F32, l2)
        lin2 = sb("lin2", [P, HW], F32, l2)
        res2 = sb("res2", [P, HW], F32, l2)
        qmax2 = sb("qmax2", [P, HT, NQ], F32, l2)
        negmax2 = sb("negmax2", [P, HT], F32, l2)
        den2 = sb("den2", [P, HT], F32, l2)
        nrm2 = sb("nrm2", [P, 3, HT], F32, l2)
        l2.close()
        l12.close()
        l3 = ExitStack()
        keys = [sb(f"keys{h}", [P, N], F32R, l3) for h in range(HEADS)]
        masks = [sb(f"mask{i}", [P, N], BF16, l3) for i in range(HT)]
        rows3 = [sb(f"rows3_{k}", [P, QW], F32, l3) for k in range(2)]
        qs = [sb(f"qs{h}", [P, HW], F32R, l3) for h in range(HEADS)]
        prep = ExitStack()
        x3t = [sb(f"x3t{b}", [D, CW], F32, prep) for b in range(2)]
        skip_out = [sb(f"skip_out{b}", [P, CW], F32, prep) for b in range(2)]
        q_out = [sb(f"q_out{b}", [P, 2, CW], F32R, prep) for b in range(2)]
        x3c = [sb(f"x3c{b}", [P, CW], F32, prep) for b in range(2)]
        prep.close()
        score = [sb(f"score{b}", [P, N], F32, l3) for b in range(2)]
        probt = sb("probt", [P, NT, HW], F32, l3)
        skip_in = sb("skip_in", [P, HW], F32, l3)
        headt = sb("headt", [P, HW], F32, l3)
        att = sb("att", [P, HW], F32, l3)
        diff = sb("diff", [P, HW], F32, l3)
        base = sb("base", [P, HW], F32, l3)
        res3 = sb("res3", [P, HW], F32, l3)
        out3 = sb("out3", [P, HW], F32, l3)
        dot_o = sb("dot_o", [P, D], F32, l3)
        qmax3 = sb("qmax3", [P, 2, NQ + 1], F32, l3)
        negmax3 = sb("negmax3", [P, 2], F32, l3)
        den3 = sb("den3", [P, HEADS, 2, HT], F32, l3)
        dsum = sb("dsum", [P, HEADS, HT], F32, l3)
        dinv = sb("dinv", [P, HEADS, HT], F32, l3)
        dots = sb("dots", [P, 5, HT], F32, l3)
        l3.close()

        x_loaded = [sem(f"x_loaded{g}") for g in range(GROUPS)]
        consts_in = sem("consts_in")
        N_CONST = 22
        passed_dve, passed_pool, passed_sp = (sem(f"passed_{e}") for e in ("dve", "pool", "sp"))
        setup_dve = sem("setup_dve")
        setup_act = sem("setup_act")
        setup_pool = sem("setup_pool")
        keep_ready = sem("keep_ready")
        cols_in = [sem(f"cols_in{g}") for g in range(GROUPS)]
        agg_mm = [sem(f"agg_mm{l}") for l in range(2)]
        part_done = sem("part_done")
        agg_out = [sem(f"agg_out{l}") for l in range(2)]
        lin_mm = [sem(f"lin_mm{l}") for l in range(2)]
        lin_chain = [sem(f"lin_chain{l}") for l in range(2)]
        rstd_pool = [sem(f"rstd_pool{l}") for l in range(4)]
        sq_done = sem("sq_done")
        rn_pool = sem("rn_pool")
        xn_done = sem("xn_done")
        xn_turn = sem("xn_turn")
        hi_done = sem("hi_done")
        lo_done = sem("lo_done")
        dis_done = sem("dis_done")

        rows2_in = [sem(f"rows2_in{i}") for i in range(HT)]
        cols2_in = [sem(f"cols2_in{k}") for k in range(4)]
        st_done = sem("st_done")
        sc2_mm = sem("sc2_mm")
        sc2_out = sem("sc2_out")
        max2 = sem("max2")
        exp2 = sem("exp2")
        nrm_chain = sem("nrm_chain")
        scaled2 = sem("scaled2")
        turn2 = sem("turn2")
        mix_done = sem("mix_done")
        mix_mm = sem("mix_mm")
        agg2_out = sem("agg2_out")
        nat2 = sem("nat2")
        fin2 = sem("fin2")
        x3_done = sem("x3_done")

        pp_mm = sem("pp_mm")
        x3c_done = sem("x3c_done")
        pp_act = sem("pp_act")
        pp_dve = sem("pp_dve")
        q_saved = [sem(f"q_saved{b}") for b in range(2)]
        skip_saved = [sem(f"skip_saved{b}") for b in range(2)]

        q_in = [sem(f"q_in{h}") for h in range(HEADS)]
        skip_loaded = sem("skip_loaded")
        rows3_in = [sem(f"rows3_in{k}") for k in range(2)]
        mask_done = sem("mask_done")
        sc3_mm = sem("sc3_mm")
        sc3_out = sem("sc3_out")
        floor_set = sem("floor_set")
        max3 = sem("max3")
        exp3 = sem("exp3")
        turn_a = sem("turn_a")
        turn_d = sem("turn_d")
        ev_a = sem("ev_a")
        ev_d = sem("ev_d")
        pv_mm = sem("pv_mm")
        headt_out = sem("headt_out")
        head_nat = sem("head_nat")
        dinv_chain = sem("dinv_chain")
        att_done = sem("att_done")
        dots_done = sem("dots_done")
        diff_pool = sem("diff_pool")
        gate_act = sem("gate_act")
        fin3 = sem("fin3")
        out_pool = sem("out_pool")
        stored = sem("stored")

        a_rows = a["adj_rows"].rearrange("(t p) m -> t p m", p=P)
        a_cols = a["adj_cols"]
        out_v = a["out"].rearrange("(c i p) d -> c p i d", p=P, i=HT)

        CHAIN01 = (23, 17)
        FIN2 = 7
        FIN3 = 8
        PPA, PPD = 6, 7
        PPM = 8

        UNITS = HT * NQ
        LAG2 = UNITS + 3
        STEPS = HEADS * HT
        QUADS = NT // 4
        take = {}
        n_act = n_dve = 0
        for s in range(STEPS):
            for q in range(QUADS):
                if q in (2, 5) or (q == 7 and s % 2 == 0):
                    take[s, q] = ("dve", n_dve)
                    n_dve += 1
                else:
                    take[s, q] = ("act", n_act)
                    n_act += 1
        assert n_act % 2 == 0

        def order(jj, s, q):
            if s < 0:
                jj, s = jj - 1, s + STEPS
            who, k = take[s, q]
            return who, (n_act if who == "act" else n_dve) * jj + k

        def used(jj, s, q):
            if s < 0:
                jj, s = jj - 1, s + STEPS
            na = max(k for (t, r), (w, k) in take.items() if w == "act" and (t, r) <= (s, q))
            nd = [k for (t, r), (w, k) in take.items() if w == "dve" and (t, r) <= (s, q)]
            return n_act * jj + na + 1, n_dve * jj + (max(nd) + 1 if nd else 0)

        def one(ap):
            return ap.rearrange("o p n -> (o p) n")

        block = ctx.enter_context(nc.Block())

        @block.sync
        def _(sp):
            def load(dst, src):
                sp.dma_start(dst, src).then_inc(consts_in, 16)

            def load_cols(j, g):
                src = a_cols[bass.ds(2 * j, 2), :, g * GT:(g + 1) * GT, :].rearrange("h p m n -> p h m n")
                sp.dma_start(cols[g][:, :, :, :], src).then_inc(cols_in[g], 16)

            for g in range(GROUPS):
                m = slice(g * GT * D, (g + 1) * GT * D)
                src = a["x"].rearrange("(t p) d -> p t d", p=P)[:, g * GT:(g + 1) * GT, :]
                sp.dma_start(xa[:, m].rearrange("p (t d) -> p t d", d=D), src).then_inc(x_loaded[g], 16)
                load_cols(0, g)
                if g == 0:
                    load(ident[:, :], a["ident"])
                    load(w0[:, :], a["w0_t"])
                    load(bias0[:, :], a["b0"].partition_broadcast(P))
                    for t, name in ((alpha0, "alpha0"), (alpha2, "alpha2"), (beta2, "beta2")):
                        load(t, a[name].partition_broadcast(P))
            load(keep_xt[:, :], a["x_t"])
            for t, name in ((stack, "stack"), (w1, "w1"), (wv, "wv"), (ws, "ws"), (wq, "wq"),
                            (bq, "bq"), (bk, "bk")):
                load(t[:, :], a[name])
            for h in range(HEADS):
                load(wk[:, h, :, :], a["wk"][:, C * h:C * h + C].rearrange("d (o c) -> d o c", o=1)
                     .broadcast_to([D, 4, C]))
            for t, name in ((bias1, "b1"), (bias_v, "bv"), (bias_s, "bs")):
                load(t[:, :], a[name].partition_broadcast(P))
            load(gate_w[:, :], a["wb"].partition_broadcast(P))
            for l in range(2):
                if l == 1:
                    for g in range(GROUPS):
                        sp.wait_ge(agg_mm[0], GROUPS * (NC - 1) + g + 1)
                        sp.wait_ge(part_done, GROUPS * (NC - 1) + g + 1)
                        load_cols(0, g)
                with sp.Fori(1, NC) as j:
                    for g in range(GROUPS):
                        sp.wait_ge(agg_mm[l], GROUPS * (j - 1) + g + 1)
                        if l == 0:
                            sp.wait_ge(part_done, GROUPS * (j - 1) + g + 1)
                        load_cols(j, g)

            def load_rows2(jj, i):
                src = one(a_rows[bass.ds(HT * jj + i, 1), :, :])
                sp.dma_start(rows2[i][:, :], src).then_inc(rows2_in[i], 16)

            def body2(jj, b):
                for u in range(UNITS):
                    if u == 0 and inside(jj, HC):
                        wait(sp, sc2_out, UNITS * jj)
                        load_rows2(jj, 1)
                    if u == NQ and inside(jj, HC) and not (isinstance(jj, int) and jj == HC - 1):
                        wait(sp, sc2_out, UNITS * jj + NQ)
                        load_rows2(jj + 1, 0)
                    if inside(jj - 1, HC):
                        n = UNITS * (jj - 1) + u
                        wait(sp, mix_done, 2 * (n - 3))
                        src = a_cols[bass.ds(jj - 1, 1), :, 4 * u:4 * u + 4, :].rearrange("o p m n -> (o p) m n")
                        sp.dma_start(cols2[u % 4][:, :, :], src).then_inc(cols2_in[u % 4], 16)

            sp.wait_ge(lo_done, NC)
            load_rows2(0, 0)
            for jj in range(2):
                body2(jj, jj)
            with sp.Fori(2, HC - 1) as jj:
                body2(jj, 0)
            for jj in (HC - 1, HC):
                body2(jj, 0)

            sp.wait_ge(x3_done, HC)
            def load_q(jj, h):
                src = q_dram[:, C * h:C * h + C, bass.ds(HW * jj, HW)]
                for pair_ in range(2):
                    dst = qs[h][2 * C * pair_:2 * C * pair_ + 2 * C, :].bitcast(F32)
                    sp.dma_start(dst, src).then_inc(q_in[h], 16)

            def load_rows3(jj, n):
                i, k = n // NQ, n % NQ
                src = one(a_rows[bass.ds(HT * jj + i, 1), :, QW * k:QW * k + QW])
                sp.dma_start(rows3[k % 2][:, :], src).then_inc(rows3_in[k % 2], 16)

            def load_skip(jj):
                src = skip_dram[bass.ds(jj, 1), :, :, :].rearrange("o p i d -> (o p) (i d)")
                sp.dma_start(skip_in[:, :], src).then_inc(skip_loaded, 16)

            for n in range(2):
                load_rows3(0, n)
            for n in range(2, HT * NQ):
                sp.wait_ge(mask_done, n - 1)
                load_rows3(0, n)
            for b in range(2):
                sp.wait_ge(q_saved[b], 16 * NC // 2)
                sp.wait_ge(skip_saved[b], 16 * 2 * NC // 2)
            for h in range(HEADS):
                load_q(0, h)
            load_skip(0)

            with sp.Fori(0, HC - 1) as jj:
                for n in range(2):
                    sp.wait_ge(mask_done, 8 * jj + n + 7)
                    load_rows3(jj + 1, n)
                for h in range(HEADS - 1):
                    sp.wait_ge(sc3_mm, NQ * (STEPS * jj + 2 * h + 2))
                    load_q(jj + 1, h)
                for n in range(2, HT * NQ):
                    sp.wait_ge(mask_done, 8 * (jj + 1) + n - 1)
                    load_rows3(jj + 1, n)
                sp.wait_ge(sc3_mm, NQ * STEPS * (jj + 1))
                load_q(jj + 1, HEADS - 1)
                sp.wait_ge(diff_pool, 2 * (jj + 1))
                apart(sp, passed_sp)
                sp.wait_ge(dots_done, 4 * (jj + 1))
                apart(sp, passed_sp)
                load_skip(jj + 1)

        @block.tensor
        def _(pe):
            for l in range(2):
                x_in, w = (xa, w0) if l == 0 else (xb, w1)
                def body(j, b, l=l, x_in=x_in, w=w):
                    if inside(j, NC):
                        wait(pe, agg_out[l], j - 1)
                        for g in range(GROUPS):
                            pe.wait_ge(cols_in[g], 16 * (j + 1 + NC * l))
                            if isinstance(j, int) and j == 0:
                                if l == 0:
                                    pe.wait_ge(x_loaded[g], 16)
                                else:
                                    pe.wait_ge(lin_chain[0], CHAIN01[0] * (g + 1) * GT // CT)
                            for m in range(GT):
                                t = g * GT + m
                                mm = pe.matmul(pair[b][:, 0:CW].rearrange("p (h n) -> p h n", h=2),
                                               x_in[:, t * D:(t + 1) * D], cols[g][:, :, m, :],
                                               start=(t == 0), stop=(t == NT - 1))
                            mm.then_inc(agg_mm[l], 1)
                    if inside(j - 1, NC):
                        o = 1 - b
                        if isinstance(j, int) and j == 1 and l == 0:
                            pe.wait_ge(consts_in, 16 * N_CONST)
                            pe.wait_ge(setup_pool, 2)
                        pe.wait_ge(agg_out[l], j)
                        wait(pe, lin_chain[l], CHAIN01[l] * (j - 2))
                        for i in range(CT):
                            mm = pe.matmul(turned[o][:, i * P:(i + 1) * P], agg[o][:, i * P:(i + 1) * P], w[:, :],
                                           start=True, stop=True)
                        if l == 0:
                            pe.wait_ge(part_done, GROUPS * j)
                            if inside(j - 2, NC):
                                pe.wait_ge(lin_chain[0], CHAIN01[0] * (j - 2) + 2)
                            for i in range(CT):
                                for g in range(GROUPS):
                                    mm = pe.matmul(sums[:, i:i + 1], part[o][:, g, i * P:(i + 1) * P], ones[:, :],
                                                   start=(g == 0), stop=(g == GROUPS - 1))
                        mm.then_inc(lin_mm[l], 1)
                    if l == 1 and inside(j - 2, NC):
                        pe.wait_ge(xn_done, CT * (j - 1))
                        wait(pe, lo_done, j - 2)
                        for i in range(CT):
                            mm = pe.transpose(turned[2][:, i * P:(i + 1) * P], xn[:, i * P:(i + 1) * P], ident[:, :])
                        mm.then_inc(xn_turn, 1)

                lagged(pe, NC, 1 + l, body)

            def turn(r, slot, v, s):
                wait(pe, mix_done, r - 1)
                for m in range(2):
                    t = 4 * v + 2 * s + m
                    for i in range(HT):
                        mm = pe.transpose(turned[slot][:, m * HW + i * P:m * HW + (i + 1) * P],
                                          prob[turn.b][i][:, t * P:(t + 1) * P], ident[:, :])
                mm.then_inc(turn2, 1)

            def mix_product(r, v, s):
                pe.wait_ge(mix_done, r + 1)
                for m in range(2):
                    t = 4 * v + 2 * s + m
                    mm = pe.matmul(sums[:, 0:HW], xa[:, t * D:(t + 1) * D], mix[(2 * v + s) % 4][:, m, :],
                                   start=(t == 0), stop=(t == NT - 1))
                mm.then_inc(mix_mm, 1)

            def body2(jj, b):
                for u in range(UNITS):
                    i, k = divmod(u, NQ)
                    tau = UNITS * jj + u
                    v = (u - LAG2) % UNITS
                    c = jj + (u - LAG2) // UNITS
                    r = 2 * (tau - LAG2)

                    def scores(half_):
                        if not inside(jj, HC):
                            return
                        if half_ == 0:
                            if u == 0:
                                pe.wait_ge(st_done, 2 * (jj + 1))
                            wait(pe, sc2_out, tau - 1)
                        m = slice(k * QW + half_ * CW, k * QW + (half_ + 1) * CW)
                        o = pair[k % 2][:, half_ * CW:(half_ + 1) * CW]
                        rows = slice(i * P, (i + 1) * P)
                        pe.matmul(o, st_hi[b][:, rows], xn_hi[:, m], start=True, stop=False)
                        pe.matmul(o, st_lo[b][:, rows], xn_hi[:, m], start=False, stop=False)
                        mm = pe.matmul(o, st_hi[b][:, rows], xn_lo[:, m], start=False, stop=True)
                        if half_ == 1:
                            mm.then_inc(sc2_mm, 1)

                    turn.b = (b + (u - LAG2) // UNITS) % 2
                    scores(0)
                    if inside(c, HC):
                        if v == 0:
                            pe.wait_ge(scaled2, HT * (c + 1))
                        turn(r, 0, v, 0)
                    if inside(c - (v == 0), HC):
                        mix_product(r - 1, (v - 1) % UNITS, 1)
                    scores(1)
                    if inside(c, HC):
                        turn(r + 1, 1, v, 1)
                        if v == 0:
                            wait(pe, agg2_out, c)
                        mix_product(r, v, 0)
                    if u == 5 and inside(jj - 2, HC):
                        pe.wait_ge(agg2_out, jj - 1)
                        wait(pe, fin2, FIN2 * (jj - 2))
                        for i2 in range(HT):
                            mm = pe.transpose(turned[2][:, i2 * P:(i2 + 1) * P], agg2[:, i2 * P:(i2 + 1) * P], ident[:, :])
                        mm.then_inc(nat2, 1)

            pe.wait_ge(lo_done, NC)
            pe.wait_ge(hi_done, NC)
            lagged(pe, HC, 2, body2)

            pe.wait_ge(x3_done, HC)
            def project(j, b):
                pe.wait_ge(x3c_done, j + 1)
                wait(pe, pp_act, PPA * (j - 1) + 1)
                for i in range(CT):
                    mm = pe.transpose(sums[:, i * P:(i + 1) * P], x3c[b][:, i * P:(i + 1) * P], ident[:, :])
                mm.then_inc(pp_mm, 1)
                pe.wait_ge(pp_act, PPA * j + 1)
                for n, (o, w) in enumerate(((turned[0], wv), (turned[1], ws))):
                    wait(pe, pp_dve, PPD * (j - 1) + n + 1)
                    for i in range(CT):
                        mm = pe.matmul(o[:, i * P:(i + 1) * P], x3t[b][:, i * P:(i + 1) * P], w[:, :],
                                       start=True, stop=True)
                    mm.then_inc(pp_mm, 1)
                wait(pe, pp_dve, PPD * (j - 1) + 3)
                pe.matmul(turned[2][:, :], wq[:, :], x3t[b][:, :], start=True, stop=True).then_inc(pp_mm, 1)
                for h in range(HEADS):
                    wait(pe, pp_dve, PPD * (j - 1) + 4 + h)
                    pe.matmul(banks[h], wk[:, h, :, :].rearrange("d a c -> d (a c)"), x3t[b][:, :],
                              start=True, stop=True).then_inc(pp_mm, 1)

            lagged(pe, NC, 0, project)

            def scores3(jj, h, i, k):
                s = STEPS * jj + HT * h + i
                if k == 0 and i == 0:
                    pe.wait_ge(q_in[h], 32 * (jj + 1))
                wait(pe, sc3_out, NQ * s + k - 1)
                for half_ in range(2):
                    m = slice(k * QW + half_ * CW, k * QW + (half_ + 1) * CW)
                    mm = pe.matmul(pair[k % 2][:, half_ * CW:(half_ + 1) * CW], qs[h][:, i * P:(i + 1) * P],
                                   keys[h][:, m], start=True, stop=True)
                mm.then_inc(sc3_mm, 1)

            def turns3(jj, s, quads):
                sg = STEPS * jj + s
                for q in quads:
                    if q % 4 == 0:
                        pe.wait_ge(exp3, 2 * sg + q // 4 + 1)
                    who, n = order(jj, s, q)
                    if who == "act":
                        slot = take[s % STEPS, q][1] % 2
                        wait(pe, ev_a, n - 1)
                    else:
                        slot = 2
                        wait(pe, ev_d, n)
                    for m in range(4):
                        t = 4 * q + m
                        mm = pe.transpose(turned[slot][:, m * P:(m + 1) * P],
                                          score[s % 2][:, t * P:(t + 1) * P], ident[:, :])
                    mm.then_inc(turn_a if who == "act" else turn_d, 1)

            def values(jj, g, quads):
                h = g % HEADS
                for q in quads:
                    if q == 0:
                        wait(pe, att_done, HT * (HEADS * jj + g))
                    ja, jd = used(jj, HT * g + 1, q)
                    pe.wait_ge(ev_a, ja)
                    wait(pe, ev_d, jd)
                    for m in range(4):
                        t = 4 * q + m
                        mm = pe.matmul(sums[C * m:C * m + C, 0:HW], xa[:, t * D + C * h:t * D + C * h + C],
                                       probt[:, t, :], start=(q == 0), stop=(q == QUADS - 1))
                    if q == QUADS - 1:
                        mm.then_inc(pv_mm, 1)

            def head_natural(jj, g):
                gg = HEADS * jj + g
                pe.wait_ge(headt_out, gg + 1)
                for i in range(HT):
                    mm = pe.matmul(sums[:, C * i:C * i + C], headt[:, i * P:(i + 1) * P], stack[:, :],
                                   start=True, stop=True)
                mm.then_inc(head_nat, 1)

            def step3(jj, s):
                h, i = divmod(s, HT)
                live = inside(jj, HC)
                first = isinstance(jj, int) and jj == 0
                turns = not (first and s < 1) and (live or s < 1)
                group = not (first and h < 1) and (live or h < 1)
                if live:
                    scores3(jj, h, i, 0)
                    scores3(jj, h, i, 1)
                if i == 1 and group:
                    values(jj, h - 1, range(4, QUADS))
                if live:
                    scores3(jj, h, i, 2)
                if turns:
                    turns3(jj, s - 1, (0, 1, 2))
                if live:
                    scores3(jj, h, i, 3)
                if turns:
                    turns3(jj, s - 1, (3,))
                for q in range(4):
                    if i == 0 and group:
                        values(jj, h - 1, (q,))
                    if turns:
                        turns3(jj, s - 1, (4 + q,))
                    if i == 1 and group and q == 0:
                        head_natural(jj, h - 1)

            pe.wait_ge(pp_act, PPA * NC)
            pe.wait_ge(pp_dve, PPD * NC)
            for s in range(STEPS):
                step3(0, s)
            with pe.Fori(1, HC) as jj:
                for s in range(STEPS):
                    step3(jj, s)
            for s in range(2):
                step3(HC, s)

        @block.scalar
        def _(act):
            act.wait_ge(consts_in, 16 * N_CONST)
            act.activation(sig_e, alpha2, ACT.Exp, scale=-1.0).then_inc(setup_act, 1)

            def body1(j, b):
                if inside(j, NC):
                    act.wait_ge(agg_mm[1], GROUPS * (j + 1))
                    wait(act, lin_mm[1], j - 1)
                    act.copy(agg[b][:, :], pair[b][:, 0:CW]).then_inc(agg_out[1], 1)
                if inside(j - 1, NC):
                    act.wait_ge(lin_chain[1], CHAIN01[1] * j)
                    wait(act, rn_pool, 2 * (j - 1))
                    for i in range(CT):
                        act.activation(sq[:, i * P:(i + 1) * P], xa[:, bass.ds(CW * (j - 1) + i * P, P)],
                                       ACT.Square, accum_out=ssq[:, 0, i:i + 1]).then_inc(sq_done, 1)
                if inside(j - 2, NC):
                    act.wait_ge(xn_turn, j - 1)
                    act.copy(xn_hi[:, bass.ds(CW * (j - 2), CW)], turned[2][:, :]).then_inc(hi_done, 1)

            lagged(act, NC, 2, body1)

            def exp_scale(jj, b, i):
                n = HT * jj + i
                act.wait_ge(max2, n + 1)
                act.activation(prob[b][i][:, :], prob[b][i][:, :], ACT.Exp, bias=negmax2[:, i:i + 1],
                               accum_out=den2[:, i:i + 1]).then_inc(exp2, 1)
                act.wait_ge(exp2, n + 1)
                act.wait_ge(nrm_chain, 3 * (n + 1))
                act.activation(prob[b][i][:, :], prob[b][i][:, :], ACT.Copy,
                               scale=nrm2[:, 2, i:i + 1]).then_inc(scaled2, 1)

            def body2(jj, b):
                if inside(jj - 1, HC):
                    exp_scale(jj - 1, 1 - b, 1)
                if inside(jj - 2, HC):
                    act.wait_ge(mix_mm, 2 * UNITS * (jj - 1))
                    wait(act, nat2, jj - 2)
                    act.copy(agg2[:, :], sums[:, 0:HW]).then_inc(agg2_out, 1)
                if inside(jj, HC):
                    exp_scale(jj, b, 0)

            lagged(act, HC, 2, body2)

            act.wait_ge(x3_done, HC)

            def project(j, b):
                wait(act, pp_mm, PPM * (j - 2) + 1)
                act.copy(x3c[b][:, :], xb[:, bass.ds(CW * j, CW)]).then_inc(x3c_done, 1)
                act.wait_ge(pp_mm, PPM * j + 1)
                wait(act, pp_mm, PPM * (j - 1))
                act.copy(x3t[b][:, :], sums[:, :]).then_inc(pp_act, 1)
                wait(act, q_saved[b], 8 * (j - b))
                act.wait_ge(pp_mm, PPM * j + 4)
                act.activation(q_out[b][:, 0, :], turned[2][:, :], ACT.Identity, bias=bq[:, :]).then_inc(pp_act, 1)
                for h in range(HEADS):
                    act.wait_ge(pp_mm, PPM * j + 5 + h)
                    act.activation(keys[h][:, bass.ds(CW * j, CW)], banks[h], ACT.Identity,
                                   bias=bk[:, h:h + 1]).then_inc(pp_act, 1)

            lagged(act, NC, 0, project)

            def exps(jj, s, half_):
                sg = STEPS * jj + s
                h, i = divmod(s % STEPS, HT)
                if half_ == 0:
                    act.wait_ge(max3, sg + 1)
                m = slice(half_ * N // 2, (half_ + 1) * N // 2)
                act.activation(score[s % 2][:, m], score[s % 2][:, m], ACT.Exp, bias=negmax3[:, s % 2:s % 2 + 1],
                               accum_out=den3[:, h, half_, i:i + 1]).then_inc(exp3, 1)

            def out_of_psum(jj, s, quads):
                for q in quads:
                    who, n = order(jj, s, q)
                    if who == "act":
                        act.wait_ge(turn_a, n + 1)
                        i = s % HT
                        act.copy(probt[:, 4 * q:4 * q + 4, i * P:(i + 1) * P],
                                 turned[take[s % STEPS, q][1] % 2][:, :].rearrange("p (m n) -> p m n", m=4))\
                            .then_inc(ev_a, 1)

            def step3(jj, s):
                h, i = divmod(s, HT)
                live = inside(jj, HC)
                first = isinstance(jj, int) and jj == 0
                if not (first and s < 1) and (live or s < 1):
                    exps(jj, s - 1, 0)
                    exps(jj, s - 1, 1)
                if i == 1 and not (first and h < 1) and (live or h < 1):
                    gg = HEADS * jj + h - 1
                    act.wait_ge(pv_mm, gg + 1)
                    wait(act, head_nat, gg)
                    act.copy(headt[:, :], sums[:, 0:HW]).then_inc(headt_out, 1)
                if not (first and s < 1) and (live or s < 1):
                    out_of_psum(jj, s - 1, range(QUADS))
                if s == 3 and not first:
                    act.wait_ge(dots_done, 4 * jj)
                    act.activation(dots[:, 2, :], dots[:, 1, :], ACT.Exp, scale=-1.0).then_inc(gate_act, 1)

            for s in range(STEPS):
                step3(0, s)
            with act.Fori(1, HC) as jj:
                for s in range(STEPS):
                    step3(jj, s)
            for s in (0, 1, 3):
                step3(HC, s)

        @block.gpsimd
        def _(pool):
            pool.memset(ones[:, :], 1.0).then_inc(setup_pool, 1)
            pool.memset(half[:, :], -0.5).then_inc(setup_pool, 1)
            pool.wait_ge(setup_pool, 2)

            def inverse_root(out, tmp, in_, least, op, n, sem_, count):
                apart(pool, passed_pool)
                pool.tensor_scalar(tmp, in_, least, None, op).then_inc(sem_, 1)
                pool.wait_ge(sem_, count + 1)
                pool.tensor_tensor(out, tmp, half[:, 0:1].to_broadcast([P, n]), ALU.pow).then_inc(sem_, 1)

            for l in range(2):
                def body(j, b, l=l):
                    if inside(j - 1, NC):
                        pool.wait_ge(lin_chain[l], CHAIN01[l] * j - 4)
                        inverse_root(rstd[:, :], var_e[:, :], mv[:, :, 1], EPS, ALU.add, CT, rstd_pool[l], 2 * (j - 1))
                        if l == 1:
                            pool.wait_ge(sq_done, CT * j)
                            inverse_root(ssq[:, 2, :], ssq[:, 1, :], ssq[:, 0, :], 1e-16, ALU.max, CT, rn_pool, 2 * (j - 1))
                lagged(pool, NC, 1, body)
                if l == 0:
                    pool.wait_ge(lin_chain[0], CHAIN01[0] * NC)
                    inverse_root(dis[:, :], dis_t[:, :], rowsum[:, :], 1.0, ALU.max, NT, dis_done, 0)

            pool.wait_ge(lo_done, NC)
            pool.wait_ge(hi_done, NC)

            def body2(jj, b):
                if inside(jj, HC):
                    wait(pool, sc2_mm, UNITS * (jj - 1))
                    pool.tensor_copy(st_hi[b][:, :], xn_hi[:, bass.ds(HW * jj, HW)].bitcast(F32)).then_inc(st_done, 1)
                    pool.tensor_copy(st_lo[b][:, :], xn_lo[:, bass.ds(HW * jj, HW)].bitcast(F32)).then_inc(st_done, 1)
                if inside(jj - 2, HC):
                    pool.wait_ge(fin2, FIN2 * (jj - 1))
                    inverse_root(rstd[:, 0:HT], var_e[:, 0:HT], mv[:, 0:HT, 1], EPS, ALU.add, HT, rstd_pool[2], 2 * (jj - 2))

            lagged(pool, HC, 2, body2)

            def store(j, b):
                pool.wait_ge(pp_dve, PPD * j + 3)
                for c in range(2):
                    dst = skip_dram[bass.ds(2 * j + c, 1), :, :, :].rearrange("o p i d -> (o p) (i d)")
                    pool.dma_start(dst, skip_out[b][:, c * HW:(c + 1) * HW]).then_inc(skip_saved[b], 16)
                pool.dma_start(q_dram[:, :, bass.ds(CW * j, CW)].rearrange("w p n -> p w n"),
                               q_out[b][:, :, :].bitcast(F32)).then_inc(q_saved[b], 16)


            def masks3(jj):
                for i in range(HT):
                    for k in range(NQ):
                        n = NQ * i + k
                        pool.wait_ge(rows3_in[k % 2], 16 * (HT * NQ // 2 * jj + n // 2 + 1))
                        wait(pool, sc3_out, NQ * (STEPS * jj - HT + i) + k + 1)
                        apart(pool, passed_pool)
                        pool.tensor_scalar(masks[i][:, k * QW:(k + 1) * QW], rows3[k % 2][:, :], 0.0, MASKED,
                                           ALU.is_equal, ALU.mult).then_inc(mask_done, 1)

            def finish3(jj):
                pool.wait_ge(att_done, HEADS * HT * (jj + 1))
                pool.wait_ge(skip_loaded, 16 * (jj + 1))
                wait(pool, fin3, FIN3 * jj)
                pool.tensor_tensor(diff[:, :], skip_in[:, :], att[:, :], ALU.subtract).then_inc(diff_pool, 1)
                pool.tensor_tensor(base[:, :], att[:, :], xb[:, bass.ds(HW * jj, HW)], ALU.add).then_inc(diff_pool, 1)
                pool.wait_ge(fin3, FIN3 * (jj + 1))
                inverse_root(rstd[:, 0:HT], var_e[:, 0:HT], mv[:, 0:HT, 1], EPS, ALU.add, HT, rstd_pool[3], 4 * jj)
                pool.wait_ge(rstd_pool[3], 4 * jj + 2)
                wait(pool, stored, 16 * jj)
                apart(pool, passed_pool)
                for i in range(HT):
                    pool.tensor_scalar(out3[:, i * P:(i + 1) * P], res3[:, i * P:(i + 1) * P], mv[:, i, 0:1],
                                       rstd[:, i:i + 1], ALU.subtract, ALU.mult).then_inc(rstd_pool[3], 1)
                pool.wait_ge(rstd_pool[3], 4 * jj + 4)
                dst = out_v[bass.ds(jj, 1), :, :, :].rearrange("o p i d -> (o p) i d")
                pool.dma_start(dst, out3[:, :].rearrange("p (i d) -> p i d", i=HT)).then_inc(stored, 16)

            pool.wait_ge(x3_done, HC)
            masks3(0)
            lagged(pool, NC, 0, store)
            masks3(1)
            with pool.Fori(1, HC - 1) as jj:
                finish3(jj - 1)
                masks3(jj + 1)
            finish3(HC - 2)
            finish3(HC - 1)
            pool.wait_ge(stored, 16 * HC)

        @block.vector
        def _(dve):
            dve.wait_ge(consts_in, 16 * N_CONST)
            for g in range(GROUPS):
                dve.wait_ge(x_loaded[g], 16)
            dve.tensor_scalar(keep0, alpha0, -1.0, 1.0, ALU.mult, ALU.add).then_inc(setup_dve, 1)
            dve.wait_ge(setup_dve, 1)
            dve.tensor_scalar(keep_xt[:, :], keep_xt[:, :], keep0, None, ALU.mult).then_inc(setup_dve, 1)
            dve.tensor_tensor(gate_out[:, :], gate_w[:, 0:D], gate_w[:, 2 * D:3 * D], ALU.add).then_inc(setup_dve, 1)
            dve.tensor_tensor(gate_skip[:, :], gate_w[:, D:2 * D], gate_w[:, 2 * D:3 * D], ALU.subtract).then_inc(setup_dve, 1)
            dve.wait_ge(setup_act, 1)
            dve.tensor_scalar(sig_d, sig_e, 1.0, None, ALU.add).then_inc(setup_dve, 1)
            dve.wait_ge(setup_dve, 5)
            dve.reciprocal(sig2, sig_d).then_inc(setup_dve, 1)
            dve.wait_ge(setup_dve, 6)
            dve.tensor_scalar(negsig2, sig2, -1.0, None, ALU.mult).then_inc(setup_dve, 1)
            dve.wait_ge(setup_dve, 7)

            for l in range(2):
                x_res, x_out = (xa, xb) if l == 0 else (xb, xa)
                chain = Chain(dve, lin_chain[l], CHAIN01[l])

                def body(j, b, l=l, x_res=x_res, x_out=x_out, chain=chain):
                    if l == 0 and inside(j, NC):
                        wait(dve, lin_mm[0], j - 1)
                        for g in range(GROUPS):
                            dve.wait_ge(cols_in[g], 16 * (j + 1))
                            dve.tensor_reduce(part[b][:, g, :].rearrange("p (h n) -> p h n", h=2),
                                              cols[g][:, :, :, :].rearrange("p h m n -> p h n m"),
                                              AX.X, ALU.add).then_inc(part_done, 1)
                        dve.wait_ge(agg_mm[0], GROUPS * (j + 1))
                        dve.scalar_tensor_tensor(agg[b][:, :], pair[b][:, 0:CW], alpha0,
                                                 keep_xt[:, bass.ds(CW * j, CW)], ALU.mult, ALU.add)\
                            .then_inc(agg_out[0], 1)
                    if inside(j - 1, NC):
                        o = 1 - b
                        chain.round(j - 1)
                        dve.wait_ge(lin_mm[l], j)
                        if l == 0:
                            chain.add(dve.tensor_copy(rowsum[:, bass.ds(CT * (j - 1), CT)], sums[:, 0:CT]))
                            chain.link(dve.tensor_scalar(deg, sums[:, 0:CT], alpha0, keep0, ALU.mult, ALU.add))
                            chain.add(dve.scalar_tensor_tensor(deg_safe, deg, 0.0, deg, ALU.is_equal, ALU.add))
                            chain.link(dve.tensor_scalar(deg_nz, deg, 0.0, None, ALU.not_equal))
                            chain.link(dve.reciprocal(deg_inv, deg_safe))
                            chain.link(dve.tensor_tensor(inv, deg_inv, deg_nz, ALU.mult))
                            for i in range(CT):
                                chain.add(dve.scalar_tensor_tensor(
                                    lin[:, i * P:(i + 1) * P], turned[o][:, i * P:(i + 1) * P], inv[:, i:i + 1],
                                    bias0[:, :], ALU.mult, ALU.add))
                        else:
                            for i in range(CT):
                                chain.add(dve.tensor_tensor(lin[:, i * P:(i + 1) * P], turned[o][:, i * P:(i + 1) * P],
                                                            bias1[:, :], ALU.add))
                        chain.sync()
                        chain.link(dve.scalar_tensor_tensor(res[:, :], lin[:, :], 0.0,
                                                            x_res[:, bass.ds(CW * (j - 1), CW)], ALU.max, ALU.add))
                        for i in range(CT):
                            chain.add(dve.bn_stats(stats[:, i, :], res[:, i * P:(i + 1) * P]))
                        chain.sync()
                        apart(dve, passed_dve)
                        for i in range(CT):
                            chain.add(dve.bn_aggr(mv[:, i, :], stats[:, i, :]))
                        dve.wait_ge(rstd_pool[l], 2 * j)
                        chain.sync()
                        for i in range(CT):
                            chain.add(dve.tensor_scalar(
                                x_out[:, bass.ds(CW * (j - 1) + i * P, P)], res[:, i * P:(i + 1) * P],
                                mv[:, i, 0:1], rstd[:, i:i + 1], ALU.subtract, ALU.mult))
                        chain.done()
                        if l == 1:
                            chain.sync()
                            dve.wait_ge(rn_pool, 2 * j)
                            wait(dve, xn_turn, j - 1)
                            for i in range(CT):
                                dve.tensor_scalar(xn[:, i * P:(i + 1) * P], xa[:, bass.ds(CW * (j - 1) + i * P, P)],
                                                  ssq[:, 2, i:i + 1], None, ALU.mult).then_inc(xn_done, 1)
                    if l == 1 and inside(j - 2, NC):
                        dve.wait_ge(hi_done, j - 1)
                        m = bass.ds(CW * (j - 2), CW)
                        dve.tensor_tensor(xn_lo[:, m], turned[2][:, :], xn_hi[:, m].bitcast(F32), ALU.subtract)\
                            .then_inc(lo_done, 1)

                lagged(dve, NC, 1 + l, body)

            dve.wait_ge(dis_done, 2)
            dve.wait_ge(lo_done, NC)
            fin = Chain(dve, fin2, FIN2)

            def mix_tiles(r, slot, v, s, c):
                dve.wait_ge(turn2, r + 1)
                dve.wait_ge(cols2_in[v % 4], 16 * (UNITS // 4 * c + v // 4 + 1))
                wait(dve, mix_mm, r - 3)
                for m in range(2):
                    t = 4 * v + 2 * s + m
                    ins = dve.scalar_tensor_tensor(mix[(2 * v + s) % 4][:, m, :], cols2[v % 4][:, 2 * s + m, :],
                                                   dis[:, t:t + 1], turned[slot][:, m * HW:(m + 1) * HW],
                                                   ALU.mult, ALU.add)
                ins.then_inc(mix_done, 1)

            def norm2(jj, i):
                n = HT * jj + i
                dve.wait_ge(exp2, n + 1)
                dve.tensor_tensor(nrm2[:, 0, i:i + 1], den2[:, i:i + 1], dis[:, bass.ds(n, 1)], ALU.mult).then_inc(nrm_chain, 1)
                dve.wait_ge(nrm_chain, 3 * n + 1)
                dve.reciprocal(nrm2[:, 1, i:i + 1], nrm2[:, 0, i:i + 1]).then_inc(nrm_chain, 1)
                dve.wait_ge(nrm_chain, 3 * n + 2)
                dve.tensor_tensor(nrm2[:, 2, i:i + 1], nrm2[:, 1, i:i + 1], sig2, ALU.mult).then_inc(nrm_chain, 1)

            def body2(jj, b):
                for u in range(UNITS):
                    i, k = divmod(u, NQ)
                    tau = UNITS * jj + u
                    v = (u - LAG2) % UNITS
                    c = jj + (u - LAG2) // UNITS
                    r = 2 * (tau - LAG2)
                    if inside(c, HC):
                        mix_tiles(r, 0, v, 0, c)
                    if u == 1 and inside(jj - 1, HC):
                        norm2(jj - 1, 1)
                    if u == 5 and inside(jj, HC):
                        norm2(jj, 0)
                    if inside(jj, HC):
                        dve.wait_ge(sc2_mm, tau + 1)
                        if k == 0:
                            dve.wait_ge(rows2_in[i], 16 * (jj + 1))
                        wait(dve, turn2, 2 * UNITS * (jj - 2) + 4 * k + 4)
                        apart(dve, passed_dve)
                        m = slice(k * QW, (k + 1) * QW)
                        dve.tensor_tensor_reduce(prob[b][i][:, m], pair[k % 2][:, :], rows2[i][:, m], beta2, -3.0e38,
                                                 ALU.mult, ALU.max, qmax2[:, i, k:k + 1]).then_inc(sc2_out, 1)
                        if k == NQ - 1:
                            dve.wait_ge(sc2_out, tau + 1)
                            dve.tensor_reduce(negmax2[:, i:i + 1], qmax2[:, i, :], AX.X, ALU.max, negate=True)\
                                .then_inc(max2, 1)
                    if inside(c, HC):
                        mix_tiles(r + 1, 1, v, 1, c)
                    if u == 6 and inside(jj - 2, HC):
                        fin.round(jj - 2)
                        dve.wait_ge(nat2, jj - 1)
                        for i2 in range(HT):
                            fin.add(dve.tensor_scalar(lin2[:, i2 * P:(i2 + 1) * P], turned[2][:, i2 * P:(i2 + 1) * P],
                                                      dis[:, bass.ds(HT * (jj - 2) + i2, 1)], None, ALU.mult))
                        fin.sync()
                        fin.link(dve.scalar_tensor_tensor(res2[:, :], xa[:, bass.ds(HW * (jj - 2), HW)], negsig2,
                                                          lin2[:, :], ALU.mult, ALU.add))
                        for i2 in range(HT):
                            fin.add(dve.bn_stats(stats[:, i2, :], res2[:, i2 * P:(i2 + 1) * P]))
                        fin.sync()
                        apart(dve, passed_dve)
                        for i2 in range(HT):
                            fin.add(dve.bn_aggr(mv[:, i2, :], stats[:, i2, :]))
                        fin.done()
                    if u == 7 and inside(jj - 2, HC):
                        dve.wait_ge(fin2, FIN2 * (jj - 1))
                        dve.wait_ge(rstd_pool[2], 2 * (jj - 1))
                        for i2 in range(HT):
                            ins = dve.tensor_scalar(xb[:, bass.ds(HW * (jj - 2) + i2 * P, P)],
                                                    res2[:, i2 * P:(i2 + 1) * P], mv[:, i2, 0:1], rstd[:, i2:i2 + 1],
                                                    ALU.subtract, ALU.mult)
                        ins.then_inc(x3_done, 1)

            lagged(dve, HC, 2, body2)

            dve.wait_ge(x3_done, HC)

            def project(j, b):
                wait(dve, skip_saved[b], 16 * (j - b))
                for n, (bias, dst) in enumerate(((bias_v, xa[:, bass.ds(CW * j, CW)]), (bias_s, skip_out[b][:, :]))):
                    dve.wait_ge(pp_mm, PPM * j + 2 + n)
                    shape = dst.rearrange("p (i d) -> p i d", d=D)
                    dve.tensor_tensor(shape, turned[n][:, :].rearrange("p (i d) -> p i d", d=D),
                                      bias[:, :].rearrange("p (o d) -> p o d", o=1).broadcast_to([P, CT, D]), ALU.add)\
                        .then_inc(pp_dve, 1)
                dve.wait_ge(pp_act, PPA * j + 2)
                dve.scalar_tensor_tensor(q_out[b][:, 1, :], turned[2][:, :], bq[:, :],
                                         q_out[b][:, 0, :].bitcast(F32), ALU.add, ALU.subtract).then_inc(pp_dve, 1)
                lo = slice(2 * C, 4 * C)
                for h in range(HEADS):
                    dve.wait_ge(pp_act, PPA * j + 3 + h)
                    kk = keys[h][lo, bass.ds(CW * j, CW)]
                    dve.scalar_tensor_tensor(kk, banks[h][lo, :], bk[lo, h:h + 1], kk.bitcast(F32),
                                             ALU.add, ALU.subtract).then_inc(pp_dve, 1)

            lagged(dve, NC, 0, project)

            for b in range(2):
                dve.wait_ge(q_saved[b], 16 * NC // 2)
                dve.wait_ge(skip_saved[b], 16 * 2 * NC // 2)
            dve.memset(qmax3[:, :, NQ:NQ + 1], FLOOR).then_inc(floor_set, 1)
            dve.wait_ge(floor_set, 1)
            fin = Chain(dve, fin3, FIN3)
            att_v = att[:, :].rearrange("p (i c h) -> p i c h", i=HT, h=HEADS)

            def masked(jj, s, k):
                h, i = divmod(s, HT)
                sg = STEPS * jj + s
                dve.wait_ge(sc3_mm, NQ * sg + k + 1)
                if h == 0:
                    dve.wait_ge(mask_done, HT * NQ * jj + NQ * i + k + 1)
                if not (isinstance(jj, int) and STEPS * jj + s < 2):
                    na, nd = used(jj, s - 2, 2 * k + 1)
                    wait(dve, turn_a, na)
                    wait(dve, turn_d, nd)
                apart(dve, passed_dve)
                m = slice(k * QW, (k + 1) * QW)
                dve.tensor_tensor_reduce(score[s % 2][:, m], pair[k % 2][:, :], masks[i][:, m], float(C) ** -0.5, -3.0e38,
                                         ALU.add, ALU.max, qmax3[:, s % 2, k:k + 1]).then_inc(sc3_out, 1)

            def out_of_psum(jj, s, q):
                if (s % STEPS, q) in take and take[s % STEPS, q][0] == "dve":
                    _, n = order(jj, s, q)
                    i = s % HT
                    dve.wait_ge(turn_d, n + 1)
                    dve.tensor_copy(probt[:, 4 * q:4 * q + 4, i * P:(i + 1) * P],
                                    turned[2][:, :].rearrange("p (m n) -> p m n", m=4)).then_inc(ev_d, 1)

            def step3(jj, s):
                h, i = divmod(s, HT)
                live = inside(jj, HC)
                first = isinstance(jj, int) and jj == 0
                turns = not (first and s < 1) and (live or s < 1)
                if live:
                    masked(jj, s, 0)
                    masked(jj, s, 1)
                    masked(jj, s, 2)
                if turns:
                    out_of_psum(jj, s - 1, 2)
                if live:
                    masked(jj, s, 3)
                    dve.wait_ge(sc3_out, NQ * (STEPS * jj + s + 1))
                    dve.tensor_reduce(negmax3[:, s % 2:s % 2 + 1], qmax3[:, s % 2, :], AX.X, ALU.max, negate=True)\
                        .then_inc(max3, 1)
                group = not (first and h < 1) and (live or h < 1)
                gg, hd = HEADS * jj + h - 1, (h - 1) % HEADS
                if i == 1 and group:
                    dve.wait_ge(exp3, 2 * HT * (gg + 1))
                    dve.scalar_tensor_tensor(dsum[:, hd, :], den3[:, hd, 0, :], 1e-30, den3[:, hd, 1, :],
                                             ALU.max, ALU.add).then_inc(dinv_chain, 1)
                if turns:
                    out_of_psum(jj, s - 1, 5)
                if i == 1 and group:
                    dve.wait_ge(dinv_chain, 2 * gg + 1)
                    dve.reciprocal(dinv[:, hd, :], dsum[:, hd, :]).then_inc(dinv_chain, 1)
                if turns:
                    out_of_psum(jj, s - 1, 7)
                if i == 1 and group:
                    dve.wait_ge(head_nat, gg + 1)
                    dve.wait_ge(dinv_chain, 2 * (gg + 1))
                    if h == 1:
                        wait(dve, diff_pool, 2 * jj)
                    for i2 in range(HT):
                        dve.tensor_scalar(att_v[:, i2, :, hd], sums[:, C * i2:C * i2 + C],
                                          dinv[:, hd, i2:i2 + 1], None, ALU.mult).then_inc(att_done, 1)
                if s == 2 and not first:
                    dve.wait_ge(att_done, HEADS * HT * jj)
                    dve.wait_ge(skip_loaded, 16 * jj)
                    for i2 in range(HT):
                        m = slice(i2 * D, (i2 + 1) * D)
                        dve.tensor_tensor_reduce(dot_o[:, :], att[:, m], gate_out[:, :], 1.0, 0.0,
                                                 ALU.mult, ALU.add, dots[:, 0, i2:i2 + 1]).then_inc(dots_done, 1)
                        dve.wait_ge(dots_done, 4 * (jj - 1) + 2 * i2 + 1)
                        dve.tensor_tensor_reduce(dot_o[:, :], skip_in[:, m], gate_skip[:, :], 1.0, dots[:, 0, i2:i2 + 1],
                                                 ALU.mult, ALU.add, dots[:, 1, i2:i2 + 1]).then_inc(dots_done, 1)
                        dve.wait_ge(dots_done, 4 * (jj - 1) + 2 * i2 + 2)
                if s == 4 and not first:
                    fin.round(jj - 1)
                    dve.wait_ge(gate_act, jj)
                    fin.link(dve.tensor_scalar(dots[:, 3, :], dots[:, 2, :], 1.0, None, ALU.add))
                    fin.link(dve.reciprocal(dots[:, 4, :], dots[:, 3, :]))
                    dve.wait_ge(diff_pool, 2 * jj)
                    wait(dve, rstd_pool[3], 4 * (jj - 1))
                    for i2 in range(HT):
                        m = slice(i2 * D, (i2 + 1) * D)
                        fin.add(dve.scalar_tensor_tensor(res3[:, m], diff[:, m], dots[:, 4, i2:i2 + 1], base[:, m],
                                                         ALU.mult, ALU.add))
                    fin.sync()
                    for i2 in range(HT):
                        fin.add(dve.bn_stats(stats[:, i2, :], res3[:, i2 * P:(i2 + 1) * P]))
                    fin.sync()
                    apart(dve, passed_dve)
                    for i2 in range(HT):
                        fin.add(dve.bn_aggr(mv[:, i2, :], stats[:, i2, :]))
                    fin.done()

            for s in range(STEPS):
                step3(0, s)
            with dve.Fori(1, HC) as jj:
                for s in range(STEPS):
                    step3(jj, s)
            for s in (0, 1, 2, 4):
                step3(HC, s)

    return nc


_OUT = (N, D)


def kernel(**inputs):
    import numpy as np
    import concourse.bacc as bacc
    from concourse.bass_utils import run_bass_kernel_spmd

    f = {k: np.asarray(v) for k, v in inputs.items()}
    adj = f["adj"]
    arrays = {
        "adj_rows": adj,
        "adj_cols": adj.reshape(HC, HW, NT, P).transpose(0, 3, 2, 1),
        "x": f["x"],
        "x_t": f["x"].T,
        "w0_t": f["L0_gnn_W"].T,
        "w1": f["L1_gnn_kernel"],
        "wv": f["L3_gnn_Wv"], "ws": f["L3_gnn_Ws"], "wq": f["L3_gnn_Wq"], "wk": f["L3_gnn_Wk"],
        "b0": f["L0_gnn_b"], "b1": f["L1_gnn_bias"], "bv": f["L3_gnn_bv"], "bs": f["L3_gnn_bs"],
        "bq": f["L3_gnn_bq"].reshape(P, 1), "bk": np.tile(f["L3_gnn_bk"].reshape(HEADS, C).T, (4, 1)),
        "wb": f["L3_gnn_Wb"].reshape(3 * D),
        "alpha0": f["L0_gnn_alpha"].reshape(1),
        "alpha2": f["L2_gnn_alpha"].reshape(1),
        "beta2": f["L2_gnn_beta"].reshape(1),
        "ident": np.eye(P, dtype=np.float32),
        "stack": np.tile(np.eye(C, dtype=np.float32), (4, 1)),
    }
    arrays = {k: np.ascontiguousarray(v) for k, v in arrays.items()}
    nc = bacc.Bacc("TRN2", target_bir_lowering=False, num_devices=1)
    args = {k: nc.dram_tensor(f"in_{k}", v.shape, mybir.dt.from_np(v.dtype), kind="ExternalInput").ap()
            for k, v in arrays.items()}
    args["out"] = nc.dram_tensor("out_x", _OUT, F32, kind="ExternalOutput").ap()
    graph_layers(nc, args)
    r = run_bass_kernel_spmd(nc, [{f"in_{k}": v for k, v in arrays.items()}], core_ids=[0])
    return r.results[0]["out_x"]
```

```python
from contextlib import ExitStack

import concourse.bass as bass
from concourse import mybir

F32 = mybir.dt.float32
F32R = mybir.dt.float32r
BF16 = mybir.dt.bfloat16
ALU = mybir.AluOpType
ACT = mybir.ActivationFunctionType
AX = mybir.AxisListType

P = 128
N = 4096
D = 128
NT = N // P
CW = 512
NC = N // CW
CT = CW // P
GROUPS = 4
GT = NT // GROUPS
HW = 256
HC = N // HW
HT = HW // P
QW = 1024
NQ = N // QW
HEADS, C = 4, 32
EPS = 1e-5
MASKED = -1.0e30
FLOOR = -1.0e29


def wait(eng, sem, value):
    if isinstance(value, int) and value <= 0:
        return
    eng.wait_ge(sem, value)


def apart(eng, passed):
    eng.sem_inc(passed, 1)


class Chain:

    def __init__(self, eng, sem, per):
        self.eng, self.sem, self.per = eng, sem, per

    def round(self, j):
        self.base, self.k = self.per * j, 0

    def add(self, ins):
        ins.then_inc(self.sem, 1)
        self.k += 1

    def sync(self):
        self.eng.wait_ge(self.sem, self.base + self.k)

    def link(self, ins):
        self.add(ins)
        self.sync()

    def done(self):
        assert self.k == self.per, (self.k, self.per)


def lagged(eng, n, lag, body):
    for j in range(2):
        body(j, j)
    with eng.Fori(1, n // 2) as t:
        for b in range(2):
            body(2 * t + b, b)
    for j in range(n, n + lag):
        body(j, j % 2)


def inside(j, n):
    return not isinstance(j, int) or 0 <= j < n


def graph_layers(nc, a):
    ctx = ExitStack()
    with ctx:
        def sem(name):
            return ctx.enter_context(nc.semaphore(name))

        def sb(name, shape, dt=F32, at=ctx):
            return at.enter_context(nc.sbuf_tensor(name, shape, dt))

        def ps(name, shape):
            return ctx.enter_context(nc.psum_tensor(name, shape, F32))

        pair = [ps(f"pair{k}", [P, QW]) for k in range(2)]
        turned = [ps(f"turned{k}", [P, CW]) for k in range(3)]
        sums = ps("sums", [P, CW])
        banks = [pair[0][:, 0:CW], pair[0][:, CW:QW], pair[1][:, 0:CW], pair[1][:, CW:QW]]

        xa = sb("xa", [P, N])
        xb = sb("xb", [P, N])
        ident = sb("ident", [P, P])
        stack = sb("stack", [P, C])
        ones = sb("ones", [P, 1])
        w0 = sb("w0", [D, D])
        w1 = sb("w1", [D, D])
        bias0 = sb("bias0", [P, D])
        bias1 = sb("bias1", [P, D])
        wq = sb("wq", [D, D])
        wk = sb("wk", [D, HEADS, 4, C])
        bq = sb("bq", [P, 1])
        bk = sb("bk", [P, HEADS])
        wv = sb("wv", [D, D])
        ws = sb("ws", [D, D])
        bias_v = sb("bias_v", [P, D])
        bias_s = sb("bias_s", [P, D])
        gate_w = sb("gate_w", [P, 3 * D])
        gate_out = sb("gate_out", [P, D])
        gate_skip = sb("gate_skip", [P, D])
        scal = sb("scal", [P, 8])
        alpha0, alpha2, beta2 = scal[:, 0:1], scal[:, 1:2], scal[:, 2:3]
        keep0, sig_e, sig_d, sig2, negsig2 = (scal[:, k:k + 1] for k in range(3, 8))
        half = sb("half", [P, 1])
        rowsum = sb("rowsum", [P, NT])
        dis_t = sb("dis_t", [P, NT])
        dis = sb("dis", [P, NT])
        stats = sb("stats", [P, CT, 6])
        mv = sb("mv", [P, CT, 2])
        var_e = sb("var_e", [P, CT])
        rstd = sb("rstd", [P, CT])
        rest_dram = nc.dram_tensor("rest_dram", (2, HC, P, HW), F32, kind="Internal").ap()
        q_dram = nc.dram_tensor("q_dram", (2, HEADS * C, N), F32, kind="Internal").ap()

        l12 = ExitStack()
        xn_hi = sb("xn_hi", [D, N], F32R, l12)
        xn_lo = sb("xn_lo", [D, N], F32R, l12)
        l01 = ExitStack()
        cols = [sb(f"cols{g}", [P, 2, GT, HW], F32, l01) for g in range(GROUPS)]
        keep_xt = sb("keep_xt", [D, N], F32, l01)
        part = [sb(f"part{b}", [P, GROUPS, CW], F32, l01) for b in range(2)]
        agg = [sb(f"agg{b}", [D, CW], F32, l01) for b in range(2)]
        lin = sb("lin", [P, CW], F32, l01)
        res = sb("res", [P, CW], F32, l01)
        xn = sb("xn", [P, CW], F32, l01)
        sq = sb("sq", [P, CW], F32, l01)
        small = sb("small", [P, 6, CT], F32, l01)
        deg, deg_safe, deg_nz, deg_inv, inv = (small[:, k, :] for k in range(5))
        ssq = sb("ssq", [P, 3, CT], F32, l01)
        l01.close()
        l2 = ExitStack()
        rows2 = [sb(f"rows2_{i}", [P, N], F32, l2) for i in range(HT)]
        cols2 = [sb(f"cols2_{k}", [P, 4, HW], F32, l2) for k in range(4)]
        prob = [[sb(f"prob{b}{i}", [P, N], F32, l2) for i in range(HT)] for b in range(2)]
        mix = [sb(f"mix{k}", [P, 2, HW], F32, l2) for k in range(4)]
        st_hi = [sb(f"st_hi{b}", [D, HW], F32R, l2) for b in range(2)]
        st_lo = [sb(f"st_lo{b}", [D, HW], F32R, l2) for b in range(2)]
        agg2 = sb("agg2", [D, HW], F32, l2)
        lin2 = sb("lin2", [P, HW], F32, l2)
        res2 = sb("res2", [P, HW], F32, l2)
        qmax2 = sb("qmax2", [P, HT, NQ], F32, l2)
        negmax2 = sb("negmax2", [P, HT], F32, l2)
        den2 = sb("den2", [P, HT], F32, l2)
        nrm2 = sb("nrm2", [P, 3, HT], F32, l2)
        l2.close()
        l12.close()
        l3 = ExitStack()
        keys = [sb(f"keys{h}", [P, N], F32R, l3) for h in range(HEADS)]
        masks = [[sb(f"mask{i}", [P, N], BF16, l3) for i in range(HT)],
                 [xb[:, i * N // 2:(i + 1) * N // 2].bitcast(BF16) for i in range(HT)]]
        rows3 = [sb(f"rows3_{k}", [P, QW], F32, l3) for k in range(2)]
        qs = [sb(f"qs{h}", [P, HW], F32R, l3) for h in range(HEADS)]
        prep = ExitStack()
        x3t = [sb(f"x3t{b}", [D, CW], F32, prep) for b in range(2)]
        skip_out = [sb(f"skip_out{b}", [P, CW], F32, prep) for b in range(2)]
        q_out = [sb(f"q_out{b}", [P, 2, CW], F32R, prep) for b in range(2)]
        x3c = [sb(f"x3c{b}", [P, CW], F32, prep) for b in range(2)]
        prep.close()
        score = [sb(f"score{b}", [P, N], F32, l3) for b in range(2)]
        probt = sb("probt", [P, NT, HW], F32, l3)
        rest_in = sb("rest_in", [P, 2, HW], F32, l3)
        skip_in, x3_in = rest_in[:, 0, :], rest_in[:, 1, :]
        headt = sb("headt", [P, HW], F32, l3)
        att = sb("att", [P, HW], F32, l3)
        diff = sb("diff", [P, HW], F32, l3)
        base = sb("base", [P, HW], F32, l3)
        res3 = sb("res3", [P, HW], F32, l3)
        out3 = sb("out3", [P, HW], F32, l3)
        dot_o = sb("dot_o", [P, D], F32, l3)
        qmax3 = sb("qmax3", [P, 2, NQ + 1], F32, l3)
        negmax3 = sb("negmax3", [P, 2], F32, l3)
        den3 = sb("den3", [P, HEADS, 2, HT], F32, l3)
        dsum = sb("dsum", [P, HEADS, HT], F32, l3)
        dinv = sb("dinv", [P, HEADS, HT], F32, l3)
        dots = sb("dots", [P, 5, HT], F32, l3)
        l3.close()

        x_loaded = [sem(f"x_loaded{g}") for g in range(GROUPS)]
        consts_in = sem("consts_in")
        N_CONST = 22
        passed_dve, passed_pool, passed_sp = (sem(f"passed_{e}") for e in ("dve", "pool", "sp"))
        setup_dve = sem("setup_dve")
        setup_act = sem("setup_act")
        setup_pool = sem("setup_pool")
        keep_ready = sem("keep_ready")
        cols_in = [sem(f"cols_in{g}") for g in range(GROUPS)]
        agg_mm = [sem(f"agg_mm{l}") for l in range(2)]
        part_done = sem("part_done")
        agg_out = [sem(f"agg_out{l}") for l in range(2)]
        lin_mm = [sem(f"lin_mm{l}") for l in range(2)]
        lin_chain = [sem(f"lin_chain{l}") for l in range(2)]
        rstd_pool = [sem(f"rstd_pool{l}") for l in range(4)]
        sq_done = sem("sq_done")
        rn_pool = sem("rn_pool")
        xn_done = sem("xn_done")
        xn_turn = sem("xn_turn")
        hi_done = sem("hi_done")
        lo_done = sem("lo_done")
        dis_done = sem("dis_done")

        rows2_in = [sem(f"rows2_in{i}") for i in range(HT)]
        cols2_in = [sem(f"cols2_in{k}") for k in range(4)]
        st_done = sem("st_done")
        sc2_mm = sem("sc2_mm")
        sc2_out = sem("sc2_out")
        max2 = sem("max2")
        exp2 = sem("exp2")
        nrm_chain = sem("nrm_chain")
        scaled2 = sem("scaled2")
        turn2 = sem("turn2")
        mix_done = sem("mix_done")
        mix_mm = sem("mix_mm")
        agg2_out = sem("agg2_out")
        nat2 = sem("nat2")
        fin2 = sem("fin2")
        x3_done = sem("x3_done")

        pp_mm = sem("pp_mm")
        x3c_done = sem("x3c_done")
        pp_act = sem("pp_act")
        pp_dve = sem("pp_dve")
        x3_saved = sem("x3_saved")
        q_saved = [sem(f"q_saved{b}") for b in range(2)]
        skip_saved = [sem(f"skip_saved{b}") for b in range(2)]

        q_in = [sem(f"q_in{h}") for h in range(HEADS)]
        rest_loaded = sem("rest_loaded")
        rows3_in = [sem(f"rows3_in{k}") for k in range(2)]
        mask_done = sem("mask_done")
        sc3_mm = sem("sc3_mm")
        sc3_out = sem("sc3_out")
        floor_set = sem("floor_set")
        max3 = sem("max3")
        exp3 = sem("exp3")
        turn_a = sem("turn_a")
        turn_d = sem("turn_d")
        ev_a = sem("ev_a")
        ev_d = sem("ev_d")
        pv_mm = sem("pv_mm")
        headt_out = sem("headt_out")
        head_nat = sem("head_nat")
        dinv_chain = sem("dinv_chain")
        att_done = sem("att_done")
        dots_done = sem("dots_done")
        diff_pool = sem("diff_pool")
        gate_act = sem("gate_act")
        fin3 = sem("fin3")
        out_pool = sem("out_pool")
        stored = sem("stored")

        a_rows = a["adj_rows"].rearrange("(t p) m -> t p m", p=P)
        a_cols = a["adj_cols"]
        out_v = a["out"].rearrange("(c i p) d -> c p i d", p=P, i=HT)

        CHAIN01 = (23, 17)
        FIN2 = 7
        FIN3 = 8
        PPA, PPD = 6, 7
        PPM = 8

        UNITS = HT * NQ
        LAG2 = UNITS + 3
        STEPS = HEADS * HT
        QUADS = NT // 4
        take = {}
        n_act = n_dve = 0
        for s in range(STEPS):
            for q in range(QUADS):
                if q in (2, 5) or (q == 7 and s % 2 == 0):
                    take[s, q] = ("dve", n_dve)
                    n_dve += 1
                else:
                    take[s, q] = ("act", n_act)
                    n_act += 1
        assert n_act % 2 == 0

        def tile(jj, s):
            return not isinstance(jj, int) or 0 <= STEPS * jj + s < STEPS * HC

        def order(jj, s, q):
            if s < 0:
                jj, s = jj - 1, s + STEPS
            who, k = take[s, q]
            return who, (n_act if who == "act" else n_dve) * jj + k

        def used(jj, s, q):
            if s < 0:
                jj, s = jj - 1, s + STEPS
            na = max(k for (t, r), (w, k) in take.items() if w == "act" and (t, r) <= (s, q))
            nd = [k for (t, r), (w, k) in take.items() if w == "dve" and (t, r) <= (s, q)]
            return n_act * jj + na + 1, n_dve * jj + (max(nd) + 1 if nd else 0)

        def one(ap):
            return ap.rearrange("o p n -> (o p) n")

        block = ctx.enter_context(nc.Block())

        @block.sync
        def _(sp):
            def load(dst, src):
                sp.dma_start(dst, src).then_inc(consts_in, 16)

            def load_cols(j, g):
                src = a_cols[bass.ds(2 * j, 2), :, g * GT:(g + 1) * GT, :].rearrange("h p m n -> p h m n")
                sp.dma_start(cols[g][:, :, :, :], src).then_inc(cols_in[g], 16)

            for g in range(GROUPS):
                m = slice(g * GT * D, (g + 1) * GT * D)
                src = a["x"].rearrange("(t p) d -> p t d", p=P)[:, g * GT:(g + 1) * GT, :]
                sp.dma_start(xa[:, m].rearrange("p (t d) -> p t d", d=D), src).then_inc(x_loaded[g], 16)
                load_cols(0, g)
                if g == 0:
                    load(ident[:, :], a["ident"])
                    load(w0[:, :], a["w0_t"])
                    load(bias0[:, :], a["b0"].partition_broadcast(P))
                    for t, name in ((alpha0, "alpha0"), (alpha2, "alpha2"), (beta2, "beta2")):
                        load(t, a[name].partition_broadcast(P))
            load(keep_xt[:, :], a["x_t"])
            for t, name in ((stack, "stack"), (w1, "w1"), (wv, "wv"), (ws, "ws"), (wq, "wq"),
                            (bq, "bq"), (bk, "bk")):
                load(t[:, :], a[name])
            for h in range(HEADS):
                load(wk[:, h, :, :], a["wk"][:, C * h:C * h + C].rearrange("d (o c) -> d o c", o=1)
                     .broadcast_to([D, 4, C]))
            for t, name in ((bias1, "b1"), (bias_v, "bv"), (bias_s, "bs")):
                load(t[:, :], a[name].partition_broadcast(P))
            load(gate_w[:, :], a["wb"].partition_broadcast(P))
            for l in range(2):
                if l == 1:
                    for g in range(GROUPS):
                        sp.wait_ge(agg_mm[0], GROUPS * (NC - 1) + g + 1)
                        sp.wait_ge(part_done, GROUPS * (NC - 1) + g + 1)
                        load_cols(0, g)
                with sp.Fori(1, NC) as j:
                    for g in range(GROUPS):
                        sp.wait_ge(agg_mm[l], GROUPS * (j - 1) + g + 1)
                        if l == 0:
                            sp.wait_ge(part_done, GROUPS * (j - 1) + g + 1)
                        load_cols(j, g)

            def load_rows2(jj, i):
                src = one(a_rows[bass.ds(HT * jj + i, 1), :, :])
                sp.dma_start(rows2[i][:, :], src).then_inc(rows2_in[i], 16)

            def body2(jj, b):
                for u in range(UNITS):
                    if u == 0 and inside(jj, HC):
                        wait(sp, sc2_out, UNITS * jj)
                        load_rows2(jj, 1)
                    if u == NQ and inside(jj, HC) and not (isinstance(jj, int) and jj == HC - 1):
                        wait(sp, sc2_out, UNITS * jj + NQ)
                        load_rows2(jj + 1, 0)
                    if inside(jj - 1, HC):
                        n = UNITS * (jj - 1) + u
                        wait(sp, mix_done, 2 * (n - 3))
                        src = a_cols[bass.ds(jj - 1, 1), :, 4 * u:4 * u + 4, :].rearrange("o p m n -> (o p) m n")
                        sp.dma_start(cols2[u % 4][:, :, :], src).then_inc(cols2_in[u % 4], 16)

            sp.wait_ge(lo_done, NC)
            load_rows2(0, 0)
            for jj in range(2):
                body2(jj, jj)
            with sp.Fori(2, HC - 1) as jj:
                body2(jj, 0)
            for jj in (HC - 1, HC):
                body2(jj, 0)

            sp.wait_ge(x3_done, HC)
            def load_q(jj, h):
                src = q_dram[:, C * h:C * h + C, bass.ds(HW * jj, HW)]
                for pair_ in range(2):
                    dst = qs[h][2 * C * pair_:2 * C * pair_ + 2 * C, :].bitcast(F32)
                    sp.dma_start(dst, src).then_inc(q_in[h], 16)

            def load_rows3(jj, n):
                i, k = n // NQ, n % NQ
                src = one(a_rows[bass.ds(HT * jj + i, 1), :, QW * k:QW * k + QW])
                sp.dma_start(rows3[k % 2][:, :], src).then_inc(rows3_in[k % 2], 16)

            def load_rest(jj):
                src = rest_dram[:, bass.ds(jj, 1), :, :].rearrange("w o p n -> (o p) w n")
                sp.dma_start(rest_in[:, :, :], src).then_inc(rest_loaded, 16)

            sp.dma_start(rest_dram[1, :, :, :].rearrange("c p n -> p c n"),
                         xb[:, :].rearrange("p (c n) -> p c n", n=HW)).then_inc(x3_saved, 16)
            for n in range(2):
                load_rows3(0, n)
            for n in range(2, HT * NQ):
                sp.wait_ge(mask_done, n - 1)
                load_rows3(0, n)
            for b in range(2):
                sp.wait_ge(q_saved[b], 16 * NC // 2)
                sp.wait_ge(skip_saved[b], 16 * 2 * NC // 2)
            for h in range(HEADS):
                load_q(0, h)
            sp.wait_ge(x3_saved, 16)
            load_rest(0)

            def step3(jj):
                for h, quarters in enumerate(((0, 1, 2, 3), (4, 5), (6, 7), ())):
                    if not (isinstance(jj, int) and jj == HC - 1):
                        for n in quarters:
                            sp.wait_ge(mask_done, HT * NQ * (jj + 1) + n - 1)
                            load_rows3(jj + 1, n)
                        sp.wait_ge(sc3_mm, NQ * (STEPS * jj + HT * (h + 1)))
                        load_q(jj + 1, h)
                    if h == 1 and not (isinstance(jj, int) and jj == 0):
                        sp.wait_ge(diff_pool, 2 * jj)
                        apart(sp, passed_sp)
                        sp.wait_ge(dots_done, 4 * jj)
                        apart(sp, passed_sp)
                        load_rest(jj)

            step3(0)
            with sp.Fori(1, HC - 1) as jj:
                step3(jj)
            step3(HC - 1)

        @block.tensor
        def _(pe):
            for l in range(2):
                x_in, w = (xa, w0) if l == 0 else (xb, w1)
                def body(j, b, l=l, x_in=x_in, w=w):
                    if inside(j, NC):
                        wait(pe, agg_out[l], j - 1)
                        for g in range(GROUPS):
                            pe.wait_ge(cols_in[g], 16 * (j + 1 + NC * l))
                            if isinstance(j, int) and j == 0:
                                if l == 0:
                                    pe.wait_ge(x_loaded[g], 16)
                                else:
                                    pe.wait_ge(lin_chain[0], CHAIN01[0] * (g + 1) * GT // CT)
                            for m in range(GT):
                                t = g * GT + m
                                mm = pe.matmul(pair[b][:, 0:CW].rearrange("p (h n) -> p h n", h=2),
                                               x_in[:, t * D:(t + 1) * D], cols[g][:, :, m, :],
                                               start=(t == 0), stop=(t == NT - 1))
                            mm.then_inc(agg_mm[l], 1)
                    if inside(j - 1, NC):
                        o = 1 - b
                        if isinstance(j, int) and j == 1 and l == 0:
                            pe.wait_ge(consts_in, 16 * N_CONST)
                            pe.wait_ge(setup_pool, 2)
                        pe.wait_ge(agg_out[l], j)
                        wait(pe, lin_chain[l], CHAIN01[l] * (j - 2))
                        for i in range(CT):
                            mm = pe.matmul(turned[o][:, i * P:(i + 1) * P], agg[o][:, i * P:(i + 1) * P], w[:, :],
                                           start=True, stop=True)
                        if l == 0:
                            pe.wait_ge(part_done, GROUPS * j)
                            if inside(j - 2, NC):
                                pe.wait_ge(lin_chain[0], CHAIN01[0] * (j - 2) + 2)
                            for i in range(CT):
                                for g in range(GROUPS):
                                    mm = pe.matmul(sums[:, i:i + 1], part[o][:, g, i * P:(i + 1) * P], ones[:, :],
                                                   start=(g == 0), stop=(g == GROUPS - 1))
                        mm.then_inc(lin_mm[l], 1)
                    if l == 1 and inside(j - 2, NC):
                        pe.wait_ge(xn_done, CT * (j - 1))
                        wait(pe, lo_done, j - 2)
                        for i in range(CT):
                            mm = pe.transpose(turned[2][:, i * P:(i + 1) * P], xn[:, i * P:(i + 1) * P], ident[:, :])
                        mm.then_inc(xn_turn, 1)

                lagged(pe, NC, 1 + l, body)

            def turn(r, slot, v, s):
                wait(pe, mix_done, r - 1)
                for m in range(2):
                    t = 4 * v + 2 * s + m
                    for i in range(HT):
                        mm = pe.transpose(turned[slot][:, m * HW + i * P:m * HW + (i + 1) * P],
                                          prob[turn.b][i][:, t * P:(t + 1) * P], ident[:, :])
                mm.then_inc(turn2, 1)

            def mix_product(r, v, s):
                pe.wait_ge(mix_done, r + 1)
                for m in range(2):
                    t = 4 * v + 2 * s + m
                    mm = pe.matmul(sums[:, 0:HW], xa[:, t * D:(t + 1) * D], mix[(2 * v + s) % 4][:, m, :],
                                   start=(t == 0), stop=(t == NT - 1))
                mm.then_inc(mix_mm, 1)

            def body2(jj, b):
                for u in range(UNITS):
                    i, k = divmod(u, NQ)
                    tau = UNITS * jj + u
                    v = (u - LAG2) % UNITS
                    c = jj + (u - LAG2) // UNITS
                    r = 2 * (tau - LAG2)

                    def scores(half_):
                        if not inside(jj, HC):
                            return
                        if half_ == 0:
                            if u == 0:
                                pe.wait_ge(st_done, 2 * (jj + 1))
                            wait(pe, sc2_out, tau - 1)
                        m = slice(k * QW + half_ * CW, k * QW + (half_ + 1) * CW)
                        o = pair[k % 2][:, half_ * CW:(half_ + 1) * CW]
                        rows = slice(i * P, (i + 1) * P)
                        pe.matmul(o, st_hi[b][:, rows], xn_hi[:, m], start=True, stop=False)
                        pe.matmul(o, st_lo[b][:, rows], xn_hi[:, m], start=False, stop=False)
                        mm = pe.matmul(o, st_hi[b][:, rows], xn_lo[:, m], start=False, stop=True)
                        if half_ == 1:
                            mm.then_inc(sc2_mm, 1)

                    turn.b = (b + (u - LAG2) // UNITS) % 2
                    scores(0)
                    if inside(c, HC):
                        if v == 0:
                            pe.wait_ge(scaled2, HT * (c + 1))
                        turn(r, 0, v, 0)
                    if inside(c - (v == 0), HC):
                        mix_product(r - 1, (v - 1) % UNITS, 1)
                    scores(1)
                    if inside(c, HC):
                        turn(r + 1, 1, v, 1)
                        if v == 0:
                            wait(pe, agg2_out, c)
                        mix_product(r, v, 0)
                    if u == 5 and inside(jj - 2, HC):
                        pe.wait_ge(agg2_out, jj - 1)
                        wait(pe, fin2, FIN2 * (jj - 2))
                        for i2 in range(HT):
                            mm = pe.transpose(turned[2][:, i2 * P:(i2 + 1) * P], agg2[:, i2 * P:(i2 + 1) * P], ident[:, :])
                        mm.then_inc(nat2, 1)

            pe.wait_ge(lo_done, NC)
            pe.wait_ge(hi_done, NC)
            lagged(pe, HC, 2, body2)

            pe.wait_ge(x3_done, HC)
            def project(j, b):
                pe.wait_ge(x3c_done, j + 1)
                wait(pe, pp_act, PPA * (j - 1) + 1)
                for i in range(CT):
                    mm = pe.transpose(sums[:, i * P:(i + 1) * P], x3c[b][:, i * P:(i + 1) * P], ident[:, :])
                mm.then_inc(pp_mm, 1)
                pe.wait_ge(pp_act, PPA * j + 1)
                for n, (o, w) in enumerate(((turned[0], wv), (turned[1], ws))):
                    wait(pe, pp_dve, PPD * (j - 1) + n + 1)
                    for i in range(CT):
                        mm = pe.matmul(o[:, i * P:(i + 1) * P], x3t[b][:, i * P:(i + 1) * P], w[:, :],
                                       start=True, stop=True)
                    mm.then_inc(pp_mm, 1)
                wait(pe, pp_dve, PPD * (j - 1) + 3)
                pe.matmul(turned[2][:, :], wq[:, :], x3t[b][:, :], start=True, stop=True).then_inc(pp_mm, 1)
                for h in range(HEADS):
                    wait(pe, pp_dve, PPD * (j - 1) + 4 + h)
                    pe.matmul(banks[h], wk[:, h, :, :].rearrange("d a c -> d (a c)"), x3t[b][:, :],
                              start=True, stop=True).then_inc(pp_mm, 1)

            lagged(pe, NC, 0, project)

            def scores3(jj, h, i, k):
                s = STEPS * jj + HT * h + i
                if k == 0 and i == 0:
                    pe.wait_ge(q_in[h], 32 * (jj + 1))
                wait(pe, sc3_out, NQ * s + k - 1)
                for half_ in range(2):
                    m = slice(k * QW + half_ * CW, k * QW + (half_ + 1) * CW)
                    mm = pe.matmul(pair[k % 2][:, half_ * CW:(half_ + 1) * CW], qs[h][:, i * P:(i + 1) * P],
                                   keys[h][:, m], start=True, stop=True)
                mm.then_inc(sc3_mm, 1)

            def turns3(jj, s, quads):
                sg = STEPS * jj + s
                for q in quads:
                    pe.wait_ge(exp3, 2 * sg + q // 4 + 1)
                    who, n = order(jj, s, q)
                    if who == "act":
                        slot = take[s % STEPS, q][1] % 2
                        wait(pe, ev_a, n - 1)
                    else:
                        slot = 2
                        wait(pe, ev_d, n)
                    for m in range(4):
                        t = 4 * q + m
                        mm = pe.transpose(turned[slot][:, m * P:(m + 1) * P],
                                          score[s % 2][:, t * P:(t + 1) * P], ident[:, :])
                    mm.then_inc(turn_a if who == "act" else turn_d, 1)

            def values(jj, g, quads):
                h = g % HEADS
                for q in quads:
                    if q == 0:
                        wait(pe, att_done, HT * (HEADS * jj + g))
                    ja, jd = used(jj, HT * g + 1, q)
                    pe.wait_ge(ev_a, ja)
                    wait(pe, ev_d, jd)
                    for m in range(4):
                        t = 4 * q + m
                        mm = pe.matmul(sums[C * m:C * m + C, 0:HW], xa[:, t * D + C * h:t * D + C * h + C],
                                       probt[:, t, :], start=(q == 0), stop=(q == QUADS - 1))
                    if q == QUADS - 1:
                        mm.then_inc(pv_mm, 1)

            def head_natural(jj, g):
                gg = HEADS * jj + g
                pe.wait_ge(headt_out, gg + 1)
                for i in range(HT):
                    mm = pe.matmul(sums[:, C * i:C * i + C], headt[:, i * P:(i + 1) * P], stack[:, :],
                                   start=True, stop=True)
                mm.then_inc(head_nat, 1)

            def step3(jj, s):
                h, i = divmod(s, HT)

                def scores(k):
                    if tile(jj, s):
                        scores3(jj, h, i, k)

                def turns(lag, quads):
                    if tile(jj, s - lag):
                        turns3(jj, s - lag, quads)

                def products(lag, quads):
                    if tile(jj, HT * (h - lag)):
                        values(jj, h - lag, quads)

                scores(0)
                turns(2, (3,))
                if i == 1:
                    products(1, (0, 1))
                turns(2, (4,))
                if i == 0:
                    products(2, (6,))
                turns(2, (5,))
                scores(1)
                if i == 0:
                    products(2, (7,))
                if i == 1:
                    products(1, (2,))
                turns(2, (6,))
                scores(2)
                if i == 1:
                    products(1, (3,))
                turns(2, (7,))
                turns(1, (0,))
                scores(3)
                turns(1, (2, 1))
                if i == 0 and tile(jj, HT * (h - 2)):
                    head_natural(jj, h - 2)
                if i == 1:
                    products(1, (4, 5))

            pe.wait_ge(pp_act, PPA * NC)
            pe.wait_ge(pp_dve, PPD * NC)
            for s in range(STEPS):
                step3(0, s)
            with pe.Fori(1, HC) as jj:
                for s in range(STEPS):
                    step3(jj, s)
            for s in range(3):
                step3(HC, s)

        @block.scalar
        def _(act):
            act.wait_ge(consts_in, 16 * N_CONST)
            act.activation(sig_e, alpha2, ACT.Exp, scale=-1.0).then_inc(setup_act, 1)

            def body1(j, b):
                if inside(j, NC):
                    act.wait_ge(agg_mm[1], GROUPS * (j + 1))
                    wait(act, lin_mm[1], j - 1)
                    act.copy(agg[b][:, :], pair[b][:, 0:CW]).then_inc(agg_out[1], 1)
                if inside(j - 1, NC):
                    act.wait_ge(lin_chain[1], CHAIN01[1] * j)
                    wait(act, rn_pool, 2 * (j - 1))
                    for i in range(CT):
                        act.activation(sq[:, i * P:(i + 1) * P], xa[:, bass.ds(CW * (j - 1) + i * P, P)],
                                       ACT.Square, accum_out=ssq[:, 0, i:i + 1]).then_inc(sq_done, 1)
                if inside(j - 2, NC):
                    act.wait_ge(xn_turn, j - 1)
                    act.copy(xn_hi[:, bass.ds(CW * (j - 2), CW)], turned[2][:, :]).then_inc(hi_done, 1)

            lagged(act, NC, 2, body1)

            def exp_scale(jj, b, i):
                n = HT * jj + i
                act.wait_ge(max2, n + 1)
                act.activation(prob[b][i][:, :], prob[b][i][:, :], ACT.Exp, bias=negmax2[:, i:i + 1],
                               accum_out=den2[:, i:i + 1]).then_inc(exp2, 1)
                act.wait_ge(exp2, n + 1)
                act.wait_ge(nrm_chain, 3 * (n + 1))
                act.activation(prob[b][i][:, :], prob[b][i][:, :], ACT.Copy,
                               scale=nrm2[:, 2, i:i + 1]).then_inc(scaled2, 1)

            def body2(jj, b):
                if inside(jj - 1, HC):
                    exp_scale(jj - 1, 1 - b, 1)
                if inside(jj - 2, HC):
                    act.wait_ge(mix_mm, 2 * UNITS * (jj - 1))
                    wait(act, nat2, jj - 2)
                    act.copy(agg2[:, :], sums[:, 0:HW]).then_inc(agg2_out, 1)
                if inside(jj, HC):
                    exp_scale(jj, b, 0)

            lagged(act, HC, 2, body2)

            act.wait_ge(x3_done, HC)

            def project(j, b):
                wait(act, pp_mm, PPM * (j - 2) + 1)
                act.copy(x3c[b][:, :], xb[:, bass.ds(CW * j, CW)]).then_inc(x3c_done, 1)
                act.wait_ge(pp_mm, PPM * j + 1)
                wait(act, pp_mm, PPM * (j - 1))
                act.copy(x3t[b][:, :], sums[:, :]).then_inc(pp_act, 1)
                wait(act, q_saved[b], 8 * (j - b))
                act.wait_ge(pp_mm, PPM * j + 4)
                act.activation(q_out[b][:, 0, :], turned[2][:, :], ACT.Identity, bias=bq[:, :]).then_inc(pp_act, 1)
                for h in range(HEADS):
                    act.wait_ge(pp_mm, PPM * j + 5 + h)
                    act.activation(keys[h][:, bass.ds(CW * j, CW)], banks[h], ACT.Identity,
                                   bias=bk[:, h:h + 1]).then_inc(pp_act, 1)

            lagged(act, NC, 0, project)

            def exps(jj, s, half_):
                sg = STEPS * jj + s
                h, i = divmod(s % STEPS, HT)
                if half_ == 0:
                    act.wait_ge(max3, sg + 1)
                m = slice(half_ * N // 2, (half_ + 1) * N // 2)
                act.activation(score[s % 2][:, m], score[s % 2][:, m], ACT.Exp, bias=negmax3[:, s % 2:s % 2 + 1],
                               accum_out=den3[:, h, half_, i:i + 1]).then_inc(exp3, 1)

            def out_of_psum(jj, s, quads):
                for q in quads:
                    who, n = order(jj, s, q)
                    if who == "act":
                        act.wait_ge(turn_a, n + 1)
                        i = s % HT
                        act.copy(probt[:, 4 * q:4 * q + 4, i * P:(i + 1) * P],
                                 turned[take[s % STEPS, q][1] % 2][:, :].rearrange("p (m n) -> p m n", m=4))\
                            .then_inc(ev_a, 1)

            def step3(jj, s):
                h, i = divmod(s, HT)
                if tile(jj, s - 1):
                    exps(jj, s - 1, 0)
                if i == 0 and tile(jj, HT * (h - 2)):
                    gg = HEADS * jj + h - 2
                    act.wait_ge(pv_mm, gg + 1)
                    wait(act, head_nat, gg)
                    act.copy(headt[:, :], sums[:, 0:HW]).then_inc(headt_out, 1)
                if tile(jj, s - 2):
                    out_of_psum(jj, s - 2, range(4, QUADS))
                if tile(jj, s - 1):
                    exps(jj, s - 1, 1)
                    out_of_psum(jj, s - 1, range(4))
                if s == 4 and tile(jj, -1):
                    act.wait_ge(dots_done, 4 * jj)
                    act.activation(dots[:, 2, :], dots[:, 1, :], ACT.Exp, scale=-1.0).then_inc(gate_act, 1)

            for s in range(STEPS):
                step3(0, s)
            with act.Fori(1, HC) as jj:
                for s in range(STEPS):
                    step3(jj, s)
            for s in (0, 1, 2, 4):
                step3(HC, s)

        @block.gpsimd
        def _(pool):
            pool.memset(ones[:, :], 1.0).then_inc(setup_pool, 1)
            pool.memset(half[:, :], -0.5).then_inc(setup_pool, 1)
            pool.wait_ge(setup_pool, 2)

            def inverse_root(out, tmp, in_, least, op, n, sem_, count):
                apart(pool, passed_pool)
                pool.tensor_scalar(tmp, in_, least, None, op).then_inc(sem_, 1)
                pool.wait_ge(sem_, count + 1)
                pool.tensor_tensor(out, tmp, half[:, 0:1].to_broadcast([P, n]), ALU.pow).then_inc(sem_, 1)

            for l in range(2):
                def body(j, b, l=l):
                    if inside(j - 1, NC):
                        pool.wait_ge(lin_chain[l], CHAIN01[l] * j - 4)
                        inverse_root(rstd[:, :], var_e[:, :], mv[:, :, 1], EPS, ALU.add, CT, rstd_pool[l], 2 * (j - 1))
                        if l == 1:
                            pool.wait_ge(sq_done, CT * j)
                            inverse_root(ssq[:, 2, :], ssq[:, 1, :], ssq[:, 0, :], 1e-16, ALU.max, CT, rn_pool, 2 * (j - 1))
                lagged(pool, NC, 1, body)
                if l == 0:
                    pool.wait_ge(lin_chain[0], CHAIN01[0] * NC)
                    inverse_root(dis[:, :], dis_t[:, :], rowsum[:, :], 1.0, ALU.max, NT, dis_done, 0)

            pool.wait_ge(lo_done, NC)
            pool.wait_ge(hi_done, NC)

            def body2(jj, b):
                if inside(jj, HC):
                    wait(pool, sc2_mm, UNITS * (jj - 1))
                    pool.tensor_copy(st_hi[b][:, :], xn_hi[:, bass.ds(HW * jj, HW)].bitcast(F32)).then_inc(st_done, 1)
                    pool.tensor_copy(st_lo[b][:, :], xn_lo[:, bass.ds(HW * jj, HW)].bitcast(F32)).then_inc(st_done, 1)
                if inside(jj - 2, HC):
                    pool.wait_ge(fin2, FIN2 * (jj - 1))
                    inverse_root(rstd[:, 0:HT], var_e[:, 0:HT], mv[:, 0:HT, 1], EPS, ALU.add, HT, rstd_pool[2], 2 * (jj - 2))

            lagged(pool, HC, 2, body2)

            def store(j, b):
                pool.wait_ge(pp_dve, PPD * j + 3)
                for c in range(2):
                    dst = one(rest_dram[0, bass.ds(2 * j + c, 1), :, :])
                    pool.dma_start(dst, skip_out[b][:, c * HW:(c + 1) * HW]).then_inc(skip_saved[b], 16)
                pool.dma_start(q_dram[:, :, bass.ds(CW * j, CW)].rearrange("w p n -> p w n"),
                               q_out[b][:, :, :].bitcast(F32)).then_inc(q_saved[b], 16)


            def masks3(jj, b, quarters):
                for n in quarters:
                    i, k = divmod(n, NQ)
                    pool.wait_ge(rows3_in[k % 2], 16 * (HT * NQ // 2 * jj + n // 2 + 1))
                    wait(pool, sc3_out, NQ * (STEPS * (jj - 1) - HT + i) + k + 1)
                    apart(pool, passed_pool)
                    pool.tensor_scalar(masks[b][i][:, k * QW:(k + 1) * QW], rows3[k % 2][:, :], 0.0, MASKED,
                                       ALU.is_equal, ALU.mult).then_inc(mask_done, 1)

            def residual3(jj):
                pool.wait_ge(att_done, HEADS * HT * (jj + 1))
                pool.wait_ge(rest_loaded, 16 * (jj + 1))
                wait(pool, fin3, FIN3 * jj)
                pool.tensor_tensor(diff[:, :], skip_in, att[:, :], ALU.subtract).then_inc(diff_pool, 1)
                pool.tensor_tensor(base[:, :], att[:, :], x3_in, ALU.add).then_inc(diff_pool, 1)

            def finish3(jj):
                pool.wait_ge(fin3, FIN3 * (jj + 1))
                inverse_root(rstd[:, 0:HT], var_e[:, 0:HT], mv[:, 0:HT, 1], EPS, ALU.add, HT, rstd_pool[3], 4 * jj)
                pool.wait_ge(rstd_pool[3], 4 * jj + 2)
                wait(pool, stored, 16 * jj)
                apart(pool, passed_pool)
                for i in range(HT):
                    pool.tensor_scalar(out3[:, i * P:(i + 1) * P], res3[:, i * P:(i + 1) * P], mv[:, i, 0:1],
                                       rstd[:, i:i + 1], ALU.subtract, ALU.mult).then_inc(rstd_pool[3], 1)
                pool.wait_ge(rstd_pool[3], 4 * jj + 4)
                dst = out_v[bass.ds(jj, 1), :, :, :].rearrange("o p i d -> (o p) i d")
                pool.dma_start(dst, out3[:, :].rearrange("p (i d) -> p i d", i=HT)).then_inc(stored, 16)

            def step3(jj, b):
                last = isinstance(jj, int) and jj >= HC - 1
                first = isinstance(jj, int) and jj == 0
                if not last:
                    masks3(jj + 1, 1 - b, range(0, 3))
                if not first:
                    residual3(jj - 1)
                if not last:
                    masks3(jj + 1, 1 - b, range(3, 6))
                if not first:
                    finish3(jj - 1)
                if not last:
                    masks3(jj + 1, 1 - b, range(6, HT * NQ))

            pool.wait_ge(x3_done, HC)
            masks3(0, 0, range(HT * NQ))
            lagged(pool, NC, 0, store)
            pool.wait_ge(x3c_done, NC)
            pool.wait_ge(x3_saved, 16)
            step3(0, 0)
            with pool.Fori(0, (HC - 2) // 2) as t:
                step3(2 * t + 1, 1)
                step3(2 * t + 2, 0)
            step3(HC - 1, 1)
            step3(HC, 0)
            pool.wait_ge(stored, 16 * HC)

        @block.vector
        def _(dve):
            dve.wait_ge(consts_in, 16 * N_CONST)
            for g in range(GROUPS):
                dve.wait_ge(x_loaded[g], 16)
            dve.tensor_scalar(keep0, alpha0, -1.0, 1.0, ALU.mult, ALU.add).then_inc(setup_dve, 1)
            dve.wait_ge(setup_dve, 1)
            dve.tensor_scalar(keep_xt[:, :], keep_xt[:, :], keep0, None, ALU.mult).then_inc(setup_dve, 1)
            dve.tensor_tensor(gate_out[:, :], gate_w[:, 0:D], gate_w[:, 2 * D:3 * D], ALU.add).then_inc(setup_dve, 1)
            dve.tensor_tensor(gate_skip[:, :], gate_w[:, D:2 * D], gate_w[:, 2 * D:3 * D], ALU.subtract).then_inc(setup_dve, 1)
            dve.wait_ge(setup_act, 1)
            dve.tensor_scalar(sig_d, sig_e, 1.0, None, ALU.add).then_inc(setup_dve, 1)
            dve.wait_ge(setup_dve, 5)
            dve.reciprocal(sig2, sig_d).then_inc(setup_dve, 1)
            dve.wait_ge(setup_dve, 6)
            dve.tensor_scalar(negsig2, sig2, -1.0, None, ALU.mult).then_inc(setup_dve, 1)
            dve.wait_ge(setup_dve, 7)

            for l in range(2):
                x_res, x_out = (xa, xb) if l == 0 else (xb, xa)
                chain = Chain(dve, lin_chain[l], CHAIN01[l])

                def body(j, b, l=l, x_res=x_res, x_out=x_out, chain=chain):
                    if l == 0 and inside(j, NC):
                        wait(dve, lin_mm[0], j - 1)
                        for g in range(GROUPS):
                            dve.wait_ge(cols_in[g], 16 * (j + 1))
                            dve.tensor_reduce(part[b][:, g, :].rearrange("p (h n) -> p h n", h=2),
                                              cols[g][:, :, :, :].rearrange("p h m n -> p h n m"),
                                              AX.X, ALU.add).then_inc(part_done, 1)
                        dve.wait_ge(agg_mm[0], GROUPS * (j + 1))
                        dve.scalar_tensor_tensor(agg[b][:, :], pair[b][:, 0:CW], alpha0,
                                                 keep_xt[:, bass.ds(CW * j, CW)], ALU.mult, ALU.add)\
                            .then_inc(agg_out[0], 1)
                    if inside(j - 1, NC):
                        o = 1 - b
                        chain.round(j - 1)
                        dve.wait_ge(lin_mm[l], j)
                        if l == 0:
                            chain.add(dve.tensor_copy(rowsum[:, bass.ds(CT * (j - 1), CT)], sums[:, 0:CT]))
                            chain.link(dve.tensor_scalar(deg, sums[:, 0:CT], alpha0, keep0, ALU.mult, ALU.add))
                            chain.add(dve.scalar_tensor_tensor(deg_safe, deg, 0.0, deg, ALU.is_equal, ALU.add))
                            chain.link(dve.tensor_scalar(deg_nz, deg, 0.0, None, ALU.not_equal))
                            chain.link(dve.reciprocal(deg_inv, deg_safe))
                            chain.link(dve.tensor_tensor(inv, deg_inv, deg_nz, ALU.mult))
                            for i in range(CT):
                                chain.add(dve.scalar_tensor_tensor(
                                    lin[:, i * P:(i + 1) * P], turned[o][:, i * P:(i + 1) * P], inv[:, i:i + 1],
                                    bias0[:, :], ALU.mult, ALU.add))
                        else:
                            for i in range(CT):
                                chain.add(dve.tensor_tensor(lin[:, i * P:(i + 1) * P], turned[o][:, i * P:(i + 1) * P],
                                                            bias1[:, :], ALU.add))
                        chain.sync()
                        chain.link(dve.scalar_tensor_tensor(res[:, :], lin[:, :], 0.0,
                                                            x_res[:, bass.ds(CW * (j - 1), CW)], ALU.max, ALU.add))
                        for i in range(CT):
                            chain.add(dve.bn_stats(stats[:, i, :], res[:, i * P:(i + 1) * P]))
                        chain.sync()
                        apart(dve, passed_dve)
                        for i in range(CT):
                            chain.add(dve.bn_aggr(mv[:, i, :], stats[:, i, :]))
                        dve.wait_ge(rstd_pool[l], 2 * j)
                        chain.sync()
                        for i in range(CT):
                            chain.add(dve.tensor_scalar(
                                x_out[:, bass.ds(CW * (j - 1) + i * P, P)], res[:, i * P:(i + 1) * P],
                                mv[:, i, 0:1], rstd[:, i:i + 1], ALU.subtract, ALU.mult))
                        chain.done()
                        if l == 1:
                            chain.sync()
                            dve.wait_ge(rn_pool, 2 * j)
                            wait(dve, xn_turn, j - 1)
                            for i in range(CT):
                                dve.tensor_scalar(xn[:, i * P:(i + 1) * P], xa[:, bass.ds(CW * (j - 1) + i * P, P)],
                                                  ssq[:, 2, i:i + 1], None, ALU.mult).then_inc(xn_done, 1)
                    if l == 1 and inside(j - 2, NC):
                        dve.wait_ge(hi_done, j - 1)
                        m = bass.ds(CW * (j - 2), CW)
                        dve.tensor_tensor(xn_lo[:, m], turned[2][:, :], xn_hi[:, m].bitcast(F32), ALU.subtract)\
                            .then_inc(lo_done, 1)

                lagged(dve, NC, 1 + l, body)

            dve.wait_ge(dis_done, 2)
            dve.wait_ge(lo_done, NC)
            fin = Chain(dve, fin2, FIN2)

            def mix_tiles(r, slot, v, s, c):
                dve.wait_ge(turn2, r + 1)
                dve.wait_ge(cols2_in[v % 4], 16 * (UNITS // 4 * c + v // 4 + 1))
                wait(dve, mix_mm, r - 3)
                for m in range(2):
                    t = 4 * v + 2 * s + m
                    ins = dve.scalar_tensor_tensor(mix[(2 * v + s) % 4][:, m, :], cols2[v % 4][:, 2 * s + m, :],
                                                   dis[:, t:t + 1], turned[slot][:, m * HW:(m + 1) * HW],
                                                   ALU.mult, ALU.add)
                ins.then_inc(mix_done, 1)

            def norm2(jj, i):
                n = HT * jj + i
                dve.wait_ge(exp2, n + 1)
                dve.tensor_tensor(nrm2[:, 0, i:i + 1], den2[:, i:i + 1], dis[:, bass.ds(n, 1)], ALU.mult).then_inc(nrm_chain, 1)
                dve.wait_ge(nrm_chain, 3 * n + 1)
                dve.reciprocal(nrm2[:, 1, i:i + 1], nrm2[:, 0, i:i + 1]).then_inc(nrm_chain, 1)
                dve.wait_ge(nrm_chain, 3 * n + 2)
                dve.tensor_tensor(nrm2[:, 2, i:i + 1], nrm2[:, 1, i:i + 1], sig2, ALU.mult).then_inc(nrm_chain, 1)

            def body2(jj, b):
                for u in range(UNITS):
                    i, k = divmod(u, NQ)
                    tau = UNITS * jj + u
                    v = (u - LAG2) % UNITS
                    c = jj + (u - LAG2) // UNITS
                    r = 2 * (tau - LAG2)
                    if inside(c, HC):
                        mix_tiles(r, 0, v, 0, c)
                    if u == 1 and inside(jj - 1, HC):
                        norm2(jj - 1, 1)
                    if u == 5 and inside(jj, HC):
                        norm2(jj, 0)
                    if inside(jj, HC):
                        dve.wait_ge(sc2_mm, tau + 1)
                        if k == 0:
                            dve.wait_ge(rows2_in[i], 16 * (jj + 1))
                        wait(dve, turn2, 2 * UNITS * (jj - 2) + 4 * k + 4)
                        apart(dve, passed_dve)
                        m = slice(k * QW, (k + 1) * QW)
                        dve.tensor_tensor_reduce(prob[b][i][:, m], pair[k % 2][:, :], rows2[i][:, m], beta2, -3.0e38,
                                                 ALU.mult, ALU.max, qmax2[:, i, k:k + 1]).then_inc(sc2_out, 1)
                        if k == NQ - 1:
                            dve.wait_ge(sc2_out, tau + 1)
                            dve.tensor_reduce(negmax2[:, i:i + 1], qmax2[:, i, :], AX.X, ALU.max, negate=True)\
                                .then_inc(max2, 1)
                    if inside(c, HC):
                        mix_tiles(r + 1, 1, v, 1, c)
                    if u == 6 and inside(jj - 2, HC):
                        fin.round(jj - 2)
                        dve.wait_ge(nat2, jj - 1)
                        for i2 in range(HT):
                            fin.add(dve.tensor_scalar(lin2[:, i2 * P:(i2 + 1) * P], turned[2][:, i2 * P:(i2 + 1) * P],
                                                      dis[:, bass.ds(HT * (jj - 2) + i2, 1)], None, ALU.mult))
                        fin.sync()
                        fin.link(dve.scalar_tensor_tensor(res2[:, :], xa[:, bass.ds(HW * (jj - 2), HW)], negsig2,
                                                          lin2[:, :], ALU.mult, ALU.add))
                        for i2 in range(HT):
                            fin.add(dve.bn_stats(stats[:, i2, :], res2[:, i2 * P:(i2 + 1) * P]))
                        fin.sync()
                        apart(dve, passed_dve)
                        for i2 in range(HT):
                            fin.add(dve.bn_aggr(mv[:, i2, :], stats[:, i2, :]))
                        fin.done()
                    if u == 7 and inside(jj - 2, HC):
                        dve.wait_ge(fin2, FIN2 * (jj - 1))
                        dve.wait_ge(rstd_pool[2], 2 * (jj - 1))
                        for i2 in range(HT):
                            ins = dve.tensor_scalar(xb[:, bass.ds(HW * (jj - 2) + i2 * P, P)],
                                                    res2[:, i2 * P:(i2 + 1) * P], mv[:, i2, 0:1], rstd[:, i2:i2 + 1],
                                                    ALU.subtract, ALU.mult)
                        ins.then_inc(x3_done, 1)

            lagged(dve, HC, 2, body2)

            dve.wait_ge(x3_done, HC)

            def project(j, b):
                wait(dve, skip_saved[b], 16 * (j - b))
                for n, (bias, dst) in enumerate(((bias_v, xa[:, bass.ds(CW * j, CW)]), (bias_s, skip_out[b][:, :]))):
                    dve.wait_ge(pp_mm, PPM * j + 2 + n)
                    shape = dst.rearrange("p (i d) -> p i d", d=D)
                    dve.tensor_tensor(shape, turned[n][:, :].rearrange("p (i d) -> p i d", d=D),
                                      bias[:, :].rearrange("p (o d) -> p o d", o=1).broadcast_to([P, CT, D]), ALU.add)\
                        .then_inc(pp_dve, 1)
                dve.wait_ge(pp_act, PPA * j + 2)
                dve.scalar_tensor_tensor(q_out[b][:, 1, :], turned[2][:, :], bq[:, :],
                                         q_out[b][:, 0, :].bitcast(F32), ALU.add, ALU.subtract).then_inc(pp_dve, 1)
                lo = slice(2 * C, 4 * C)
                for h in range(HEADS):
                    dve.wait_ge(pp_act, PPA * j + 3 + h)
                    kk = keys[h][lo, bass.ds(CW * j, CW)]
                    dve.scalar_tensor_tensor(kk, banks[h][lo, :], bk[lo, h:h + 1], kk.bitcast(F32),
                                             ALU.add, ALU.subtract).then_inc(pp_dve, 1)

            lagged(dve, NC, 0, project)

            for b in range(2):
                dve.wait_ge(q_saved[b], 16 * NC // 2)
                dve.wait_ge(skip_saved[b], 16 * 2 * NC // 2)
            dve.memset(qmax3[:, :, NQ:NQ + 1], FLOOR).then_inc(floor_set, 1)
            dve.wait_ge(floor_set, 1)
            fin = Chain(dve, fin3, FIN3)
            att_v = att[:, :].rearrange("p (i c h) -> p i c h", i=HT, h=HEADS)

            def masked(jj, b, s, k):
                h, i = divmod(s, HT)
                sg = STEPS * jj + s
                dve.wait_ge(sc3_mm, NQ * sg + k + 1)
                if h == 0:
                    dve.wait_ge(mask_done, HT * NQ * jj + NQ * i + k + 1)
                if not (isinstance(jj, int) and STEPS * jj + s < 2):
                    na, nd = used(jj, s - 2, 2 * k + 1)
                    wait(dve, turn_a, na)
                    wait(dve, turn_d, nd)
                apart(dve, passed_dve)
                m = slice(k * QW, (k + 1) * QW)
                dve.tensor_tensor_reduce(score[s % 2][:, m], pair[k % 2][:, :], masks[b][i][:, m], float(C) ** -0.5, -3.0e38,
                                         ALU.add, ALU.max, qmax3[:, s % 2, k:k + 1]).then_inc(sc3_out, 1)

            def out_of_psum(jj, s, q):
                if (s % STEPS, q) in take and take[s % STEPS, q][0] == "dve":
                    _, n = order(jj, s, q)
                    i = s % HT
                    dve.wait_ge(turn_d, n + 1)
                    dve.tensor_copy(probt[:, 4 * q:4 * q + 4, i * P:(i + 1) * P],
                                    turned[2][:, :].rearrange("p (m n) -> p m n", m=4)).then_inc(ev_d, 1)

            def step3(jj, b, s):
                h, i = divmod(s, HT)
                live = tile(jj, s)

                def out(lag, q):
                    if tile(jj, s - lag):
                        out_of_psum(jj, s - lag, q)

                group = i == 0 and tile(jj, HT * (h - 2))
                gg, hd = HEADS * jj + h - 2, (h - 2) % HEADS
                if live:
                    masked(jj, b, s, 0)
                out(2, 5)
                if group:
                    dve.wait_ge(exp3, 2 * HT * (gg + 1))
                    dve.scalar_tensor_tensor(dsum[:, hd, :], den3[:, hd, 0, :], 1e-30, den3[:, hd, 1, :],
                                             ALU.max, ALU.add).then_inc(dinv_chain, 1)
                if live:
                    masked(jj, b, s, 1)
                if group:
                    dve.wait_ge(dinv_chain, 2 * gg + 1)
                    dve.reciprocal(dinv[:, hd, :], dsum[:, hd, :]).then_inc(dinv_chain, 1)
                out(2, 7)
                if live:
                    masked(jj, b, s, 2)
                out(1, 2)
                if group:
                    dve.wait_ge(head_nat, gg + 1)
                    dve.wait_ge(dinv_chain, 2 * (gg + 1))
                    if hd == 0:
                        wait(dve, diff_pool, 2 * jj)
                    for i2 in range(HT):
                        dve.tensor_scalar(att_v[:, i2, :, hd], sums[:, C * i2:C * i2 + C],
                                          dinv[:, hd, i2:i2 + 1], None, ALU.mult).then_inc(att_done, 1)
                if live:
                    masked(jj, b, s, 3)
                    dve.wait_ge(sc3_out, NQ * (STEPS * jj + s + 1))
                    dve.tensor_reduce(negmax3[:, s % 2:s % 2 + 1], qmax3[:, s % 2, :], AX.X, ALU.max, negate=True)\
                        .then_inc(max3, 1)
                if s == 3 and tile(jj, -1):
                    dve.wait_ge(att_done, HEADS * HT * jj)
                    dve.wait_ge(rest_loaded, 16 * jj)
                    for i2 in range(HT):
                        m = slice(i2 * D, (i2 + 1) * D)
                        dve.tensor_tensor_reduce(dot_o[:, :], att[:, m], gate_out[:, :], 1.0, 0.0,
                                                 ALU.mult, ALU.add, dots[:, 0, i2:i2 + 1]).then_inc(dots_done, 1)
                        dve.wait_ge(dots_done, 4 * (jj - 1) + 2 * i2 + 1)
                        dve.tensor_tensor_reduce(dot_o[:, :], rest_in[:, 0, m], gate_skip[:, :], 1.0, dots[:, 0, i2:i2 + 1],
                                                 ALU.mult, ALU.add, dots[:, 1, i2:i2 + 1]).then_inc(dots_done, 1)
                        dve.wait_ge(dots_done, 4 * (jj - 1) + 2 * i2 + 2)
                if s == 5 and tile(jj, -1):
                    fin.round(jj - 1)
                    dve.wait_ge(gate_act, jj)
                    fin.link(dve.tensor_scalar(dots[:, 3, :], dots[:, 2, :], 1.0, None, ALU.add))
                    fin.link(dve.reciprocal(dots[:, 4, :], dots[:, 3, :]))
                    dve.wait_ge(diff_pool, 2 * jj)
                    wait(dve, rstd_pool[3], 4 * (jj - 1))
                    for i2 in range(HT):
                        m = slice(i2 * D, (i2 + 1) * D)
                        fin.add(dve.scalar_tensor_tensor(res3[:, m], diff[:, m], dots[:, 4, i2:i2 + 1], base[:, m],
                                                         ALU.mult, ALU.add))
                    fin.sync()
                    for i2 in range(HT):
                        fin.add(dve.bn_stats(stats[:, i2, :], res3[:, i2 * P:(i2 + 1) * P]))
                    fin.sync()
                    apart(dve, passed_dve)
                    for i2 in range(HT):
                        fin.add(dve.bn_aggr(mv[:, i2, :], stats[:, i2, :]))
                    fin.done()

            for jj in range(2):
                for s in range(STEPS):
                    step3(jj, jj, s)
            with dve.Fori(1, HC // 2) as t:
                for b in range(2):
                    for s in range(STEPS):
                        step3(2 * t + b, b, s)
            for s in (0, 1, 2, 3, 5):
                step3(HC, 0, s)

    return nc


_OUT = (N, D)


def kernel(**inputs):
    import numpy as np
    import concourse.bacc as bacc
    from concourse.bass_utils import run_bass_kernel_spmd

    f = {k: np.asarray(v) for k, v in inputs.items()}
    adj = f["adj"]
    arrays = {
        "adj_rows": adj,
        "adj_cols": adj.reshape(HC, HW, NT, P).transpose(0, 3, 2, 1),
        "x": f["x"],
        "x_t": f["x"].T,
        "w0_t": f["L0_gnn_W"].T,
        "w1": f["L1_gnn_kernel"],
        "wv": f["L3_gnn_Wv"], "ws": f["L3_gnn_Ws"], "wq": f["L3_gnn_Wq"], "wk": f["L3_gnn_Wk"],
        "b0": f["L0_gnn_b"], "b1": f["L1_gnn_bias"], "bv": f["L3_gnn_bv"], "bs": f["L3_gnn_bs"],
        "bq": f["L3_gnn_bq"].reshape(P, 1), "bk": np.tile(f["L3_gnn_bk"].reshape(HEADS, C).T, (4, 1)),
        "wb": f["L3_gnn_Wb"].reshape(3 * D),
        "alpha0": f["L0_gnn_alpha"].reshape(1),
        "alpha2": f["L2_gnn_alpha"].reshape(1),
        "beta2": f["L2_gnn_beta"].reshape(1),
        "ident": np.eye(P, dtype=np.float32),
        "stack": np.tile(np.eye(C, dtype=np.float32), (4, 1)),
    }
    arrays = {k: np.ascontiguousarray(v) for k, v in arrays.items()}
    nc = bacc.Bacc("TRN2", target_bir_lowering=False, num_devices=1)
    args = {k: nc.dram_tensor(f"in_{k}", v.shape, mybir.dt.from_np(v.dtype), kind="ExternalInput").ap()
            for k, v in arrays.items()}
    args["out"] = nc.dram_tensor("out_x", _OUT, F32, kind="ExternalOutput").ap()
    graph_layers(nc, args)
    r = run_bass_kernel_spmd(nc, [{f"in_{k}": v for k, v in arrays.items()}], core_ids=[0])
    return r.results[0]["out_x"]
```

```python
from contextlib import ExitStack

import concourse.bass as bass
from concourse import mybir

F32 = mybir.dt.float32
F32R = mybir.dt.float32r
BF16 = mybir.dt.bfloat16
ALU = mybir.AluOpType
ACT = mybir.ActivationFunctionType
AX = mybir.AxisListType

P = 128
N = 4096
D = 128
NT = N // P
CW = 512
NC = N // CW
CT = CW // P
GROUPS = 4
GT = NT // GROUPS
HW = 256
HC = N // HW
HT = HW // P
QW = 1024
NQ = N // QW
HEADS, C = 4, 32
EPS = 1e-5
MASKED = -1.0e30
FLOOR = -1.0e29


def wait(eng, sem, value):
    if isinstance(value, int) and value <= 0:
        return
    eng.wait_ge(sem, value)


def apart(eng, passed):
    eng.sem_inc(passed, 1)


class Chain:

    def __init__(self, eng, sem, per):
        self.eng, self.sem, self.per = eng, sem, per

    def round(self, j):
        self.base, self.k = self.per * j, 0

    def add(self, ins):
        ins.then_inc(self.sem, 1)
        self.k += 1

    def sync(self):
        self.eng.wait_ge(self.sem, self.base + self.k)

    def link(self, ins):
        self.add(ins)
        self.sync()

    def done(self):
        assert self.k == self.per, (self.k, self.per)


def lagged(eng, n, lag, body, first=2):
    for j in range(first):
        body(j, j % 2)
    with eng.Fori(first // 2, n // 2) as t:
        for b in range(2):
            body(2 * t + b, b)
    for j in range(n, n + lag):
        body(j, j % 2)


def inside(j, n):
    return not isinstance(j, int) or 0 <= j < n


def graph_layers(nc, a):
    ctx = ExitStack()
    with ctx:
        def sem(name):
            return ctx.enter_context(nc.semaphore(name))

        def sb(name, shape, dt=F32, at=ctx):
            return at.enter_context(nc.sbuf_tensor(name, shape, dt))

        def ps(name, shape):
            return ctx.enter_context(nc.psum_tensor(name, shape, F32))

        pair = [ps(f"pair{k}", [P, QW]) for k in range(2)]
        turned = [ps(f"turned{k}", [P, CW]) for k in range(3)]
        sums = ps("sums", [P, CW])
        mix_sums = [sums, turned[2]]
        banks = [pair[0][:, 0:CW], pair[0][:, CW:QW], pair[1][:, 0:CW], pair[1][:, CW:QW]]

        xa = sb("xa", [P, N])
        xb = sb("xb", [P, N])
        ident = sb("ident", [P, P])
        stack = sb("stack", [P, C])
        ones = sb("ones", [P, 1])
        w0 = sb("w0", [D, D])
        w1 = sb("w1", [D, D])
        bias0 = sb("bias0", [P, D])
        bias1 = sb("bias1", [P, D])
        wq = sb("wq", [D, D])
        wk = sb("wk", [D, D])
        bq = sb("bq", [P, 1])
        bk = sb("bk", [P, 1])
        wv = sb("wv", [D, D])
        ws = sb("ws", [D, D])
        bias_v = sb("bias_v", [P, D])
        bias_s = sb("bias_s", [P, D])
        gate_w = sb("gate_w", [P, 3 * D])
        gate_out = sb("gate_out", [P, D])
        gate_skip = sb("gate_skip", [P, D])
        scal = sb("scal", [P, 8])
        alpha0, alpha2, beta2 = scal[:, 0:1], scal[:, 1:2], scal[:, 2:3]
        keep0, sig_e, sig_d, sig2, negsig2 = (scal[:, k:k + 1] for k in range(3, 8))
        half = sb("half", [P, 1])
        rowsum = sb("rowsum", [P, NT])
        dis_t = sb("dis_t", [P, NT])
        dis = sb("dis", [P, NT])
        stats = sb("stats", [P, CT, 6])
        mv = sb("mv", [P, CT, 2])
        var_e = sb("var_e", [P, CT])
        rstd = sb("rstd", [P, CT])
        rest_dram = nc.dram_tensor("rest_dram", (2, HC, P, HW), F32, kind="Internal").ap()
        q_dram = nc.dram_tensor("q_dram", (2, HEADS * C, N), F32, kind="Internal").ap()

        l12 = ExitStack()
        xn_hi = sb("xn_hi", [D, N], F32R, l12)
        xn_lo = sb("xn_lo", [D, N], F32R, l12)
        l01 = ExitStack()
        cols = [sb(f"cols{g}", [P, 2, GT, HW], F32, l01) for g in range(GROUPS)]
        keep_xt = sb("keep_xt", [D, N], F32, l01)
        part = [sb(f"part{b}", [P, GROUPS, CW], F32, l01) for b in range(2)]
        agg = [sb(f"agg{b}", [D, CW], F32, l01) for b in range(2)]
        lin = sb("lin", [P, CW], F32, l01)
        res = sb("res", [P, CW], F32, l01)
        xn = sb("xn", [P, CW], F32, l01)
        sq = sb("sq", [P, CW], F32, l01)
        small = sb("small", [P, 6, CT], F32, l01)
        deg, deg_safe, deg_nz, deg_inv, inv = (small[:, k, :] for k in range(5))
        ssq = sb("ssq", [P, 3, CT], F32, l01)
        l01.close()
        l2 = ExitStack()
        rows2 = [sb(f"rows2_{i}", [P, N], F32, l2) for i in range(HT)]
        cols2 = [sb(f"cols2_{k}", [P, 4, HW], F32, l2) for k in range(4)]
        prob = [[sb(f"prob{b}{i}", [P, N], F32, l2) for i in range(HT)] for b in range(2)]
        mix = [sb(f"mix{k}", [P, 2, HW], F32, l2) for k in range(4)]
        st_hi = [sb(f"st_hi{b}", [D, HW], F32R, l2) for b in range(2)]
        st_lo = [sb(f"st_lo{b}", [D, HW], F32R, l2) for b in range(2)]
        agg2 = sb("agg2", [D, HW], F32, l2)
        lin2 = sb("lin2", [P, HW], F32, l2)
        res2 = sb("res2", [P, HW], F32, l2)
        qmax2 = sb("qmax2", [P, HT, NQ], F32, l2)
        negmax2 = sb("negmax2", [P, HT], F32, l2)
        den2 = sb("den2", [P, HT], F32, l2)
        nrm2 = sb("nrm2", [P, 3, HT], F32, l2)
        l2.close()
        l12.close()
        l3 = ExitStack()
        keys = [sb(f"keys{h}", [P, N], F32R, l3) for h in range(HEADS)]
        masks = [[sb(f"mask{i}", [P, N], BF16, l3) for i in range(HT)],
                 [xb[:, i * N // 2:(i + 1) * N // 2].bitcast(BF16) for i in range(HT)]]
        rows3 = [sb(f"rows3_{k}", [P, QW], F32, l3) for k in range(2)]
        qs = [sb(f"qs{h}", [P, HW], F32R, l3) for h in range(HEADS)]
        score = [sb(f"score{b}", [P, N], F32, l3) for b in range(2)]
        prep = ExitStack()
        x3t = [sb(f"x3t{b}", [D, CW], F32, prep) for b in range(2)]
        skip_out = [sb(f"skip_out{b}", [P, CW], F32, prep) for b in range(2)]
        q_out = [sb(f"q_out{b}", [P, 2, CW], F32R, prep) for b in range(2)]
        x3c = [sb(f"x3c{b}", [P, CW], F32, prep) for b in range(2)]
        k_out = [sb(f"k_out{b}", [P, 2, CW], F32R, prep) for b in range(2)]
        spread_f = sb("spread_f", [P, HEADS, 2, P], F32, prep)
        spread = sb("spread", [P, HEADS, 2, P], F32R, prep)
        prep.close()
        probt = sb("probt", [P, NT, HW], F32, l3)
        rest_in = sb("rest_in", [P, 2, HW], F32, l3)
        skip_in, x3_in = rest_in[:, 0, :], rest_in[:, 1, :]
        headt = sb("headt", [P, HW], F32, l3)
        att = sb("att", [P, HW], F32, l3)
        diff = sb("diff", [P, HW], F32, l3)
        base = sb("base", [P, HW], F32, l3)
        res3 = sb("res3", [P, HW], F32, l3)
        out3 = sb("out3", [P, HW], F32, l3)
        dot_o = sb("dot_o", [P, D], F32, l3)
        qmax3 = sb("qmax3", [P, 2, NQ + 1], F32, l3)
        negmax3 = sb("negmax3", [P, 2], F32, l3)
        den3 = sb("den3", [P, HEADS, 2, HT], F32, l3)
        dsum = sb("dsum", [P, HEADS, HT], F32, l3)
        dinv = sb("dinv", [P, HEADS, HT], F32, l3)
        dots = sb("dots", [P, 5, HT], F32, l3)
        l3.close()

        x_loaded = [sem(f"x_loaded{g}") for g in range(GROUPS)]
        early_in = sem("early_in")
        N_EARLY = 3
        alpha0_in = sem("alpha0_in")
        late_in = sem("late_in")
        N_LATE = 14
        keep_in = sem("keep_in")
        passed_dve, passed_pool, passed_sp = (sem(f"passed_{e}") for e in ("dve", "pool", "sp"))
        setup_dve = sem("setup_dve")
        setup_act = sem("setup_act")
        setup_pool = sem("setup_pool")
        keep_ready = sem("keep_ready")
        cols_in = [sem(f"cols_in{g}") for g in range(GROUPS)]
        agg_mm = [sem(f"agg_mm{l}") for l in range(2)]
        part_done = sem("part_done")
        part_added = sem("part_added")
        agg_out = [sem(f"agg_out{l}") for l in range(2)]
        lin_mm = [sem(f"lin_mm{l}") for l in range(2)]
        lin_chain = [sem(f"lin_chain{l}") for l in range(2)]
        rstd_pool = [sem(f"rstd_pool{l}") for l in range(4)]
        sq_done = sem("sq_done")
        rn_pool = sem("rn_pool")
        xn_done = sem("xn_done")
        xn_turn = sem("xn_turn")
        hi_done = sem("hi_done")
        lo_done = sem("lo_done")
        dis_done = sem("dis_done")

        rows2_in = [sem(f"rows2_in{i}") for i in range(HT)]
        cols2_in = [sem(f"cols2_in{k}") for k in range(4)]
        st_done = sem("st_done")
        sc2_mm = sem("sc2_mm")
        sc2_out = sem("sc2_out")
        max2 = sem("max2")
        exp2 = sem("exp2")
        nrm_chain = sem("nrm_chain")
        scaled2 = sem("scaled2")
        turn2 = sem("turn2")
        mix_done = sem("mix_done")
        mix_mm = sem("mix_mm")
        agg2_out = sem("agg2_out")
        nat2 = sem("nat2")
        fin2 = sem("fin2")
        x3_done = sem("x3_done")

        pp_mm = sem("pp_mm")
        spread_in = sem("spread_in")
        spread_done = sem("spread_done")
        x3_turn = sem("x3_turn")
        x3t_done = sem("x3t_done")
        x3c_done = sem("x3c_done")
        pp_act = sem("pp_act")
        pp_dve = sem("pp_dve")
        x3_saved = sem("x3_saved")
        q_saved = [sem(f"q_saved{b}") for b in range(2)]
        skip_saved = [sem(f"skip_saved{b}") for b in range(2)]

        q_in = [sem(f"q_in{h}") for h in range(HEADS)]
        rest_loaded = sem("rest_loaded")
        rows3_in = [sem(f"rows3_in{k}") for k in range(2)]
        mask_done = sem("mask_done")
        sc3_mm = sem("sc3_mm")
        sc3_out = sem("sc3_out")
        floor_set = sem("floor_set")
        max3 = sem("max3")
        exp3 = sem("exp3")
        turn_a = sem("turn_a")
        turn_d = sem("turn_d")
        ev_a = sem("ev_a")
        ev_d = sem("ev_d")
        pv_mm = sem("pv_mm")
        headt_out = sem("headt_out")
        head_nat = sem("head_nat")
        dinv_chain = sem("dinv_chain")
        att_done = sem("att_done")
        dots_done = sem("dots_done")
        diff_pool = sem("diff_pool")
        gate_act = sem("gate_act")
        fin3 = sem("fin3")
        out_pool = sem("out_pool")
        stored = sem("stored")

        a_rows = a["adj_rows"].rearrange("(t p) m -> t p m", p=P)
        a_cols = a["adj_cols"]
        out_v = a["out"].rearrange("(c i p) d -> c p i d", p=P, i=HT)

        CHAIN01 = (23, 17)
        FIN2 = 7
        FIN3 = 8
        PPA, PPD = 4, 6
        PPM = 8

        UNITS = HT * NQ
        LAG2 = UNITS + 3
        EARLY2 = NQ - 1
        STEPS = HEADS * HT
        QUADS = NT // 4
        take = {}
        n_act = n_dve = 0
        for s in range(STEPS):
            for q in range(QUADS):
                if q in (2, 5) or (q == 7 and s % 2 == 0):
                    take[s, q] = ("dve", n_dve)
                    n_dve += 1
                else:
                    take[s, q] = ("act", n_act)
                    n_act += 1
        assert n_act % 2 == 0

        def tile(jj, s):
            return not isinstance(jj, int) or 0 <= STEPS * jj + s < STEPS * HC

        def order(jj, s, q):
            if s < 0:
                jj, s = jj - 1, s + STEPS
            who, k = take[s, q]
            return who, (n_act if who == "act" else n_dve) * jj + k

        def counts(jj, tiles, quads):
            at = {}
            for s in tiles:
                for q in quads:
                    who, n = order(jj, s, q)
                    at[who] = n + 1
            return at

        def projections_over(eng):
            eng.wait_ge(pp_mm, PPM * NC)
            for b in range(2):
                eng.wait_ge(q_saved[b], 16 * NC // 2)
                eng.wait_ge(skip_saved[b], 16 * 2 * NC // 2)

        def one(ap):
            return ap.rearrange("o p n -> (o p) n")

        block = ctx.enter_context(nc.Block())

        @block.sync
        def _(sp):
            def load_early(dst, src):
                sp.dma_start(dst, src).then_inc(early_in, 16)

            def load_late(dst, src):
                sp.dma_start(dst, src).then_inc(late_in, 16)

            def load_cols(j, g):
                src = a_cols[bass.ds(2 * j, 2), :, g * GT:(g + 1) * GT, :].rearrange("h p m n -> p h m n")
                sp.dma_start(cols[g][:, :, :, :], src).then_inc(cols_in[g], 16)

            def load_keep(j):
                m = bass.ds(CW * j, CW)
                sp.dma_start(keep_xt[:, m], a["x_t"][:, m]).then_inc(keep_in, 16)

            sp.dma_start(alpha0, a["alpha0"].partition_broadcast(P)).then_inc(alpha0_in, 16)
            for g in range(GROUPS):
                m = slice(g * GT * D, (g + 1) * GT * D)
                src = a["x"].rearrange("(t p) d -> p t d", p=P)[:, g * GT:(g + 1) * GT, :]
                sp.dma_start(xa[:, m].rearrange("p (t d) -> p t d", d=D), src).then_inc(x_loaded[g], 16)
                load_cols(0, g)
            load_keep(0)
            load_early(ident[:, :], a["ident"])
            load_early(w0[:, :], a["w0_t"])
            load_early(bias0[:, :], a["b0"].partition_broadcast(P))
            for l in range(2):
                if l == 1:
                    for t, name in ((stack, "stack"), (w1, "w1"), (wv, "wv"), (ws, "ws"), (wq, "wq"),
                                    (wk, "wk"), (bq, "bq"), (bk, "bk")):
                        load_late(t[:, :], a[name])
                    for t, name in ((bias1, "b1"), (bias_v, "bv"), (bias_s, "bs")):
                        load_late(t[:, :], a[name].partition_broadcast(P))
                    load_late(gate_w[:, :], a["wb"].partition_broadcast(P))
                    for t, name in ((alpha2, "alpha2"), (beta2, "beta2")):
                        load_late(t, a[name].partition_broadcast(P))
                    for g in range(GROUPS):
                        sp.wait_ge(agg_mm[0], GROUPS * (NC - 1) + g + 1)
                        sp.wait_ge(part_done, GROUPS * (NC - 1) + g + 1)
                        load_cols(0, g)
                with sp.Fori(1, NC) as j:
                    for g in range(GROUPS):
                        sp.wait_ge(agg_mm[l], GROUPS * (j - 1) + g + 1)
                        if l == 0:
                            sp.wait_ge(part_done, GROUPS * (j - 1) + g + 1)
                        load_cols(j, g)
                    if l == 0:
                        sp.wait_ge(keep_ready, j)
                        load_keep(j)

            def load_rows2(jj, i):
                src = one(a_rows[bass.ds(HT * jj + i, 1), :, :])
                sp.dma_start(rows2[i][:, :], src).then_inc(rows2_in[i], 16)

            def body2(jj, b):
                for u in range(UNITS):
                    if u == 0 and inside(jj, HC) and not (isinstance(jj, int) and jj == 0):
                        wait(sp, sc2_out, UNITS * jj)
                        load_rows2(jj, 1)
                    if u == NQ and inside(jj, HC) and not (isinstance(jj, int) and jj == HC - 1):
                        wait(sp, sc2_out, UNITS * jj + NQ)
                        load_rows2(jj + 1, 0)
                    if inside(jj - 1, HC):
                        n = UNITS * (jj - 1) + u
                        wait(sp, mix_done, 2 * (n - 3))
                        src = a_cols[bass.ds(jj - 1, 1), :, 4 * u:4 * u + 4, :].rearrange("o p m n -> (o p) m n")
                        sp.dma_start(cols2[u % 4][:, :, :], src).then_inc(cols2_in[u % 4], 16)

            for i in range(HT):
                sp.wait_ge(agg_mm[1], GROUPS * (NC - 1) + i + 1)
                load_rows2(0, i)
            sp.wait_ge(agg_mm[1], GROUPS * NC)
            for jj in range(2):
                body2(jj, jj)
            with sp.Fori(2, HC - 1) as jj:
                body2(jj, 0)
            for jj in (HC - 1, HC):
                body2(jj, 0)

            sp.wait_ge(turn2, 2 * UNITS * HC)
            def load_q(jj, h):
                src = q_dram[:, C * h:C * h + C, bass.ds(HW * jj, HW)]
                for pair_ in range(2):
                    dst = qs[h][2 * C * pair_:2 * C * pair_ + 2 * C, :].bitcast(F32)
                    sp.dma_start(dst, src).then_inc(q_in[h], 16)

            def load_rows3(jj, n):
                i, k = n // NQ, n % NQ
                src = one(a_rows[bass.ds(HT * jj + i, 1), :, QW * k:QW * k + QW])
                sp.dma_start(rows3[k % 2][:, :], src).then_inc(rows3_in[k % 2], 16)

            def load_rest(jj):
                src = rest_dram[:, bass.ds(jj, 1), :, :].rearrange("w o p n -> (o p) w n")
                sp.dma_start(rest_in[:, :, :], src).then_inc(rest_loaded, 16)

            for n in range(2):
                load_rows3(0, n)
            sp.wait_ge(x3_done, HC)
            sp.dma_start(spread_f[:, :, :, :], a["spread"]).then_inc(spread_in, 16)
            sp.dma_start(rest_dram[1, :, :, :].rearrange("c p n -> p c n"),
                         xb[:, :].rearrange("p (c n) -> p c n", n=HW)).then_inc(x3_saved, 16)
            for j in range(NC):
                b = j % 2
                if j + 2 < HT * NQ:
                    sp.wait_ge(mask_done, j + 1)
                    load_rows3(0, j + 2)
                sp.wait_ge(pp_dve, PPD * j + 4)
                for c in range(2):
                    dst = one(rest_dram[0, 2 * j + c:2 * j + c + 1, :, :])
                    sp.dma_start(dst, skip_out[b][:, c * HW:(c + 1) * HW]).then_inc(skip_saved[b], 16)
                sp.dma_start(q_dram[:, :, CW * j:CW * j + CW].rearrange("w p n -> p w n"),
                             q_out[b][:, :, :].bitcast(F32)).then_inc(q_saved[b], 16)
                if j == 1:
                    sp.wait_ge(q_saved[0], 16)
                    for h in range(HEADS):
                        load_q(0, h)
            projections_over(sp)
            sp.wait_ge(x3_saved, 16)
            load_rest(0)

            def step3(jj):
                for h, quarters in enumerate(((0, 1, 2, 3), (4, 5), (6, 7), ())):
                    if not (isinstance(jj, int) and jj == HC - 1):
                        for n in quarters:
                            sp.wait_ge(mask_done, HT * NQ * (jj + 1) + n - 1)
                            load_rows3(jj + 1, n)
                        sp.wait_ge(sc3_mm, NQ * (STEPS * jj + HT * (h + 1)))
                        load_q(jj + 1, h)
                    if h == 1 and not (isinstance(jj, int) and jj == 0):
                        sp.wait_ge(diff_pool, 2 * jj)
                        apart(sp, passed_sp)
                        sp.wait_ge(dots_done, 4 * jj)
                        apart(sp, passed_sp)
                        load_rest(jj)

            step3(0)
            with sp.Fori(1, HC - 1) as jj:
                step3(jj)
            step3(HC - 1)

        @block.tensor
        def _(pe):
            def scores2(jj, b, u, half_):
                i, k = divmod(u, NQ)
                if half_ == 0:
                    if u == 0:
                        pe.wait_ge(st_done, 2 * (jj + 1))
                    wait(pe, sc2_out, UNITS * jj + u - 1)
                m = slice(k * QW + half_ * CW, k * QW + (half_ + 1) * CW)
                o = pair[k % 2][:, half_ * CW:(half_ + 1) * CW]
                rows = slice(i * P, (i + 1) * P)
                pe.matmul(o, st_hi[b][:, rows], xn_hi[:, m], start=True, stop=False)
                pe.matmul(o, st_lo[b][:, rows], xn_hi[:, m], start=False, stop=False)
                mm = pe.matmul(o, st_hi[b][:, rows], xn_lo[:, m], start=False, stop=True)
                if half_ == 1:
                    mm.then_inc(sc2_mm, 1)

            for l in range(2):
                x_in, w = (xa, w0) if l == 0 else (xb, w1)
                def body(j, b, l=l, x_in=x_in, w=w):
                    def aggregate(groups):
                        if not inside(j, NC):
                            return
                        for g in groups:
                            if g == 0:
                                wait(pe, agg_out[l], j - 1)
                            pe.wait_ge(cols_in[g], 16 * (j + 1 + NC * l))
                            if isinstance(j, int) and j == 0:
                                if l == 0:
                                    pe.wait_ge(x_loaded[g], 16)
                                else:
                                    pe.wait_ge(lin_chain[0], CHAIN01[0] * (g + 1) * GT // CT)
                            for m in range(GT):
                                t = g * GT + m
                                mm = pe.matmul(pair[b][:, 0:CW].rearrange("p (h n) -> p h n", h=2),
                                               x_in[:, t * D:(t + 1) * D], cols[g][:, :, m, :],
                                               start=(t == 0), stop=(t == NT - 1))
                            mm.then_inc(agg_mm[l], 1)

                    aggregate((0,))
                    if inside(j - 1, NC):
                        o = 1 - b
                        if isinstance(j, int) and j == 1:
                            if l == 0:
                                pe.wait_ge(early_in, 16 * N_EARLY)
                                pe.wait_ge(setup_pool, 2)
                            else:
                                pe.wait_ge(late_in, 16 * N_LATE)
                        pe.wait_ge(agg_out[l], j)
                        wait(pe, lin_chain[l], CHAIN01[l] * (j - 2))
                        for i in range(CT):
                            mm = pe.matmul(turned[o][:, i * P:(i + 1) * P], agg[o][:, i * P:(i + 1) * P], w[:, :],
                                           start=True, stop=True)
                        if l == 0:
                            pe.wait_ge(part_added, (GROUPS - 1) * j)
                            if inside(j - 2, NC):
                                pe.wait_ge(lin_chain[0], CHAIN01[0] * (j - 2) + 2)
                            for i in range(CT):
                                mm = pe.matmul(sums[:, i:i + 1], part[o][:, 0, i * P:(i + 1) * P], ones[:, :],
                                               start=True, stop=True)
                        mm.then_inc(lin_mm[l], 1)
                    aggregate(range(1, GROUPS))
                    if l == 1 and inside(j - 1, NC):
                        wait(pe, lo_done, j - 1)
                        if isinstance(j, int) and j == NC:
                            for u in range(EARLY2):
                                scores2(0, 0, u, 0)
                                scores2(0, 0, u, 1)
                        pe.wait_ge(xn_done, CT * j)
                        for i in range(CT):
                            mm = pe.transpose(turned[2][:, i * P:(i + 1) * P], xn[:, i * P:(i + 1) * P], ident[:, :])
                        mm.then_inc(xn_turn, 1)

                lagged(pe, NC, 1, body)

            def turn(r, slot, v, s, b):
                wait(pe, mix_done, r - 1)
                for m in range(2):
                    t = 4 * v + 2 * s + m
                    for i in range(HT):
                        mm = pe.transpose(turned[slot][:, m * HW + i * P:m * HW + (i + 1) * P],
                                          prob[b][i][:, t * P:(t + 1) * P], ident[:, :])
                mm.then_inc(turn2, 1)

            def mix_product(r, v, s, b):
                pe.wait_ge(mix_done, r + 1)
                for m in range(2):
                    t = 4 * v + 2 * s + m
                    mm = pe.matmul(mix_sums[b][:, 0:HW], xa[:, t * D:(t + 1) * D], mix[(2 * v + s) % 4][:, m, :],
                                   start=(t == 0), stop=(t == NT - 1))
                mm.then_inc(mix_mm, 1)

            def body2(jj, b):
                for u in range(UNITS):
                    i, k = divmod(u, NQ)
                    tau = UNITS * jj + u
                    v = (u - LAG2) % UNITS
                    c = jj + (u - LAG2) // UNITS
                    r = 2 * (tau - LAG2)

                    def scores(half_):
                        if inside(jj, HC) and not (isinstance(jj, int) and tau < EARLY2):
                            scores2(jj, b, u, half_)

                    parity = (b + (u - LAG2) // UNITS) % 2
                    scores(0)
                    if inside(c, HC):
                        if v == 0:
                            pe.wait_ge(scaled2, HT * (c + 1))
                        turn(r, 0, v, 0, parity)
                    before = inside(c - (v == 0), HC)
                    if before:
                        if v == 1:
                            wait(pe, fin2, FIN2 * (c - 1))
                        mix_product(r - 2, (v - 1) % UNITS, 0, (parity + (v == 0)) % 2)
                    scores(1)
                    if inside(c, HC):
                        turn(r + 1, 1, v, 1, parity)
                    if before:
                        mix_product(r - 1, (v - 1) % UNITS, 1, (parity + (v == 0)) % 2)
                    if u == 5 and inside(jj - 2, HC):
                        pe.wait_ge(agg2_out, jj - 1)
                        for i2 in range(HT):
                            mm = pe.transpose(mix_sums[b][:, i2 * P:(i2 + 1) * P], agg2[:, i2 * P:(i2 + 1) * P], ident[:, :])
                        mm.then_inc(nat2, 1)

            pe.wait_ge(lo_done, NC)
            pe.wait_ge(hi_done, NC)
            lagged(pe, HC, 2, body2)

            pe.wait_ge(fin2, FIN2 * (HC - 1))
            def project(j, b):
                c = 1 - b

                def rows(o, w, taken):
                    wait(pe, pp_dve, PPD * (j - 2) + taken)
                    for i in range(CT):
                        mm = pe.matmul(o[:, i * P:(i + 1) * P], x3t[c][:, i * P:(i + 1) * P], w[:, :],
                                       start=True, stop=True)
                    mm.then_inc(pp_mm, 1)

                if inside(j - 1, NC):
                    pe.wait_ge(x3t_done, j)
                    rows(turned[0], wv, 4)
                    if isinstance(j, int) and j == 1:
                        pe.wait_ge(fin2, FIN2 * HC)
                    wait(pe, pp_dve, PPD * (j - 2) + 2)
                    pe.matmul(turned[2][:, :], wk[:, :], x3t[c][:, :], start=True, stop=True).then_inc(pp_mm, 1)
                    rows(turned[1], ws, 3)
                if inside(j, NC):
                    pe.wait_ge(x3c_done, j + 1)
                    wait(pe, x3t_done, j)
                    for i in range(CT):
                        mm = pe.transpose(sums[:, i * P:(i + 1) * P], x3c[b][:, i * P:(i + 1) * P], ident[:, :])
                    mm.then_inc(x3_turn, 1)
                if inside(j - 1, NC):
                    pe.wait_ge(pp_dve, PPD * (j - 1) + 1)
                    pe.matmul(turned[0][:, :], wq[:, :], x3t[c][:, :], start=True, stop=True).then_inc(pp_mm, 1)
                    if isinstance(j, int) and j == 1:
                        pe.wait_ge(spread_done, 1)
                    pe.wait_ge(pp_dve, PPD * (j - 1) + 2)
                    for h in range(HEADS):
                        if h < 2:
                            wait(pe, pp_act, PPA * (j - 2) + 3 + h)
                        else:
                            wait(pe, pp_dve, PPD * (j - 2) + 3 + h)
                        for w in range(2):
                            mm = pe.matmul(banks[h], spread[:, h, w, :], k_out[c][:, w, :], start=(w == 0), stop=(w == 1))
                        mm.then_inc(pp_mm, 1)

            lagged(pe, NC, 1, project)

            def scores3(jj, h, i, k):
                s = STEPS * jj + HT * h + i
                if k == 0 and i == 0:
                    pe.wait_ge(q_in[h], 32 * (jj + 1))
                wait(pe, sc3_out, NQ * s + k - 1)
                for half_ in range(2):
                    m = slice(k * QW + half_ * CW, k * QW + (half_ + 1) * CW)
                    mm = pe.matmul(pair[k % 2][:, half_ * CW:(half_ + 1) * CW], qs[h][:, i * P:(i + 1) * P],
                                   keys[h][:, m], start=True, stop=True)
                mm.then_inc(sc3_mm, 1)

            def turns3(jj, s, quads):
                sg = STEPS * jj + s
                for q in quads:
                    if q % 4 == 0:
                        pe.wait_ge(exp3, 2 * sg + q // 4 + 1)
                    who, n = order(jj, s, q)
                    if who == "act":
                        slot = take[s % STEPS, q][1] % 2
                        wait(pe, ev_a, n - 1)
                    else:
                        slot = 2
                        wait(pe, ev_d, n)
                    for m in range(4):
                        t = 4 * q + m
                        mm = pe.transpose(turned[slot][:, m * P:(m + 1) * P],
                                          score[s % 2][:, t * P:(t + 1) * P], ident[:, :])
                    mm.then_inc(turn_a if who == "act" else turn_d, 1)

            def values(jj, g, quads):
                h = g % HEADS
                for q in quads:
                    if q == 0:
                        wait(pe, att_done, HT * (HEADS * jj + g))
                    at = counts(jj, (HT * g, HT * g + 1), (q,))
                    if "act" in at:
                        pe.wait_ge(ev_a, at["act"])
                    if "dve" in at:
                        pe.wait_ge(ev_d, at["dve"])
                    for m in range(4):
                        t = 4 * q + m
                        mm = pe.matmul(sums[C * m:C * m + C, 0:HW], xa[:, t * D + C * h:t * D + C * h + C],
                                       probt[:, t, :], start=(q == 0), stop=(q == QUADS - 1))
                    if q == QUADS - 1:
                        mm.then_inc(pv_mm, 1)

            def head_natural(jj, g):
                gg = HEADS * jj + g
                pe.wait_ge(headt_out, gg + 1)
                for i in range(HT):
                    mm = pe.matmul(sums[:, C * i:C * i + C], headt[:, i * P:(i + 1) * P], stack[:, :],
                                   start=True, stop=True)
                mm.then_inc(head_nat, 1)

            def step3(jj, s):
                h, i = divmod(s, HT)

                def scores(k):
                    if tile(jj, s):
                        scores3(jj, h, i, k)

                def turns(lag, quads):
                    if tile(jj, s - lag):
                        turns3(jj, s - lag, quads)

                def products(lag, quads):
                    if tile(jj, HT * (h - lag)):
                        values(jj, h - lag, quads)

                scores(0)
                turns(2, (3,))
                if i == 1:
                    products(1, (0, 1))
                turns(2, (4,))
                if i == 0:
                    products(2, (6,))
                turns(2, (5,))
                scores(1)
                if i == 0:
                    products(2, (7,))
                if i == 1:
                    products(1, (2,))
                turns(2, (6,))
                scores(2)
                if i == 1:
                    products(1, (3,))
                turns(2, (7,))
                turns(1, (0,))
                scores(3)
                turns(1, (2,))
                if i == 0 and tile(jj, HT * (h - 2)):
                    head_natural(jj, h - 2)
                turns(1, (1,))
                if i == 1:
                    products(1, (4, 5))

            pe.wait_ge(pp_act, PPA * NC)
            pe.wait_ge(pp_dve, PPD * NC)
            for s in range(STEPS):
                step3(0, s)
            with pe.Fori(1, HC) as jj:
                for s in range(STEPS):
                    step3(jj, s)
            for s in range(3):
                step3(HC, s)

        @block.scalar
        def _(act):
            def body0(j, b):
                act.wait_ge(keep_in, 16 * (j + 1))
                if isinstance(j, int) and j == 0:
                    act.wait_ge(setup_dve, 1)
                m = bass.ds(CW * j, CW)
                act.activation(keep_xt[:, m], keep_xt[:, m], ACT.Copy, scale=keep0).then_inc(keep_ready, 1)

            lagged(act, NC, 0, body0)

            act.wait_ge(late_in, 16 * N_LATE)
            act.activation(sig_e, alpha2, ACT.Exp, scale=-1.0).then_inc(setup_act, 1)

            def body1(j, b):
                if inside(j - 1, NC):
                    act.wait_ge(lin_chain[1], CHAIN01[1] * j)
                    wait(act, rn_pool, 2 * (j - 1))
                    for i in range(CT):
                        act.activation(sq[:, i * P:(i + 1) * P], xa[:, bass.ds(CW * (j - 1) + i * P, P)],
                                       ACT.Square, accum_out=ssq[:, 0, i:i + 1]).then_inc(sq_done, 1)
                if inside(j, NC):
                    act.wait_ge(agg_mm[1], GROUPS * (j + 1))
                    wait(act, lin_mm[1], j - 1)
                    act.copy(agg[b][:, :], pair[b][:, 0:CW]).then_inc(agg_out[1], 1)
                if inside(j - 1, NC):
                    act.wait_ge(xn_turn, j)
                    act.copy(xn_hi[:, bass.ds(CW * (j - 1), CW)], turned[2][:, :]).then_inc(hi_done, 1)

            lagged(act, NC, 1, body1)

            def exp_scale(jj, b, i):
                n = HT * jj + i
                act.wait_ge(max2, n + 1)
                act.activation(prob[b][i][:, :], prob[b][i][:, :], ACT.Exp, bias=negmax2[:, i:i + 1],
                               accum_out=den2[:, i:i + 1]).then_inc(exp2, 1)
                act.wait_ge(exp2, n + 1)
                act.wait_ge(nrm_chain, 3 * (n + 1))
                act.activation(prob[b][i][:, :], prob[b][i][:, :], ACT.Copy,
                               scale=nrm2[:, 2, i:i + 1]).then_inc(scaled2, 1)

            def body2(jj, b):
                if inside(jj - 1, HC):
                    exp_scale(jj - 1, 1 - b, 1)
                if inside(jj - 2, HC):
                    act.wait_ge(mix_mm, 2 * UNITS * (jj - 1))
                    wait(act, nat2, jj - 2)
                    act.copy(agg2[:, :], mix_sums[b][:, 0:HW]).then_inc(agg2_out, 1)
                if inside(jj, HC):
                    exp_scale(jj, b, 0)

            lagged(act, HC, 2, body2)

            act.wait_ge(turn2, 2 * UNITS * HC)

            def project(j, b):
                if inside(j, NC):
                    act.wait_ge(x3_done, HC // NC * (j + 1))
                    wait(act, x3_turn, j - 1)
                    act.copy(x3c[b][:, :], xb[:, bass.ds(CW * j, CW)]).then_inc(x3c_done, 1)
                c = 1 - b
                if inside(j - 1, NC):
                    wait(act, pp_mm, PPM * (j - 2))
                    act.wait_ge(pp_mm, PPM * (j - 1) + 2)
                    act.activation(k_out[c][:, 0, :], turned[2][:, :], ACT.Identity, bias=bk[:, :]).then_inc(pp_act, 1)
                if isinstance(j, int) and j == 1:
                    act.wait_ge(spread_in, 16)
                    act.copy(spread[:, :, :, :], spread_f[:, :, :, :]).then_inc(spread_done, 1)
                if inside(j, NC):
                    act.wait_ge(x3_turn, j + 1)
                    wait(act, pp_mm, PPM * (j - 1))
                    act.copy(x3t[b][:, :], sums[:, :]).then_inc(x3t_done, 1)
                if inside(j - 1, NC):
                    wait(act, q_saved[c], 8 * (j - 1 - c))
                    act.wait_ge(pp_mm, PPM * (j - 1) + 4)
                    act.activation(q_out[c][:, 0, :], turned[0][:, :], ACT.Identity, bias=bq[:, :]).then_inc(pp_act, 1)
                    for h in range(2):
                        act.wait_ge(pp_mm, PPM * (j - 1) + 5 + h)
                        act.copy(keys[h][:, bass.ds(CW * (j - 1), CW)], banks[h]).then_inc(pp_act, 1)

            lagged(act, NC, 1, project)

            def exps(jj, s, half_):
                sg = STEPS * jj + s
                h, i = divmod(s % STEPS, HT)
                if half_ == 0:
                    act.wait_ge(max3, sg + 1)
                m = slice(half_ * N // 2, (half_ + 1) * N // 2)
                act.activation(score[s % 2][:, m], score[s % 2][:, m], ACT.Exp, bias=negmax3[:, s % 2:s % 2 + 1],
                               accum_out=den3[:, h, half_, i:i + 1]).then_inc(exp3, 1)

            def out_of_psum(jj, s, quads):
                for q in quads:
                    who, n = order(jj, s, q)
                    if who == "act":
                        act.wait_ge(turn_a, n + 1)
                        i = s % HT
                        act.copy(probt[:, 4 * q:4 * q + 4, i * P:(i + 1) * P],
                                 turned[take[s % STEPS, q][1] % 2][:, :].rearrange("p (m n) -> p m n", m=4))\
                            .then_inc(ev_a, 1)

            def step3(jj, s):
                h, i = divmod(s, HT)
                if tile(jj, s - 1):
                    exps(jj, s - 1, 0)
                if i == 0 and tile(jj, HT * (h - 2)):
                    gg = HEADS * jj + h - 2
                    act.wait_ge(pv_mm, gg + 1)
                    wait(act, head_nat, gg)
                    act.copy(headt[:, :], sums[:, 0:HW]).then_inc(headt_out, 1)
                if tile(jj, s - 2):
                    out_of_psum(jj, s - 2, range(4, QUADS))
                if tile(jj, s - 1):
                    exps(jj, s - 1, 1)
                    if isinstance(jj, int) and (jj, s) == (0, 1):
                        projections_over(act)
                    out_of_psum(jj, s - 1, range(4))
                if s == 4 and tile(jj, -1):
                    act.wait_ge(dots_done, 4 * jj)
                    act.activation(dots[:, 2, :], dots[:, 1, :], ACT.Exp, scale=-1.0).then_inc(gate_act, 1)

            for s in range(STEPS):
                step3(0, s)
            with act.Fori(1, HC) as jj:
                for s in range(STEPS):
                    step3(jj, s)
            for s in (0, 1, 2, 4):
                step3(HC, s)

        @block.gpsimd
        def _(pool):
            pool.memset(ones[:, :], 1.0).then_inc(setup_pool, 1)
            pool.memset(half[:, :], -0.5).then_inc(setup_pool, 1)
            pool.wait_ge(setup_pool, 2)

            def inverse_root(out, tmp, in_, least, op, n, sem_, count):
                apart(pool, passed_pool)
                pool.tensor_scalar(tmp, in_, least, None, op).then_inc(sem_, 1)
                pool.wait_ge(sem_, count + 1)
                pool.tensor_tensor(out, tmp, half[:, 0:1].to_broadcast([P, n]), ALU.pow).then_inc(sem_, 1)

            def stationary2(jj, b):
                wait(pool, sc2_mm, UNITS * (jj - 1))
                pool.tensor_copy(st_hi[b][:, :], xn_hi[:, bass.ds(HW * jj, HW)].bitcast(F32)).then_inc(st_done, 1)
                pool.tensor_copy(st_lo[b][:, :], xn_lo[:, bass.ds(HW * jj, HW)].bitcast(F32)).then_inc(st_done, 1)

            for l in range(2):
                def body(j, b, l=l):
                    def add_sums(groups):
                        if l == 0 and inside(j, NC):
                            for g in groups:
                                pool.wait_ge(part_done, GROUPS * j + g + 1)
                                if g > 1:
                                    pool.wait_ge(part_added, (GROUPS - 1) * j + g - 1)
                                pool.tensor_tensor(part[b][:, 0, :], part[b][:, 0, :], part[b][:, g, :], ALU.add)\
                                    .then_inc(part_added, 1)

                    if l == 1 and isinstance(j, int) and j == NC:
                        pool.wait_ge(hi_done, 1)
                        pool.wait_ge(lo_done, 1)
                        stationary2(0, 0)
                    add_sums((1,))
                    if inside(j - 1, NC):
                        pool.wait_ge(lin_chain[l], CHAIN01[l] * j - 4)
                        inverse_root(rstd[:, :], var_e[:, :], mv[:, :, 1], EPS, ALU.add, CT, rstd_pool[l], 2 * (j - 1))
                        if l == 1:
                            pool.wait_ge(sq_done, CT * j)
                            inverse_root(ssq[:, 2, :], ssq[:, 1, :], ssq[:, 0, :], 1e-16, ALU.max, CT, rn_pool, 2 * (j - 1))
                    add_sums((2, 3))
                lagged(pool, NC, 1, body)
                if l == 0:
                    pool.wait_ge(lin_chain[0], CHAIN01[0] * NC)
                    inverse_root(dis[:, :], dis_t[:, :], rowsum[:, :], 1.0, ALU.max, NT, dis_done, 0)

            def body2(jj, b):
                if inside(jj, HC) and not (isinstance(jj, int) and jj == 0):
                    stationary2(jj, b)
                if inside(jj - 3, HC):
                    pool.wait_ge(fin2, FIN2 * (jj - 2))
                    inverse_root(rstd[:, 0:HT], var_e[:, 0:HT], mv[:, 0:HT, 1], EPS, ALU.add, HT, rstd_pool[2], 2 * (jj - 3))

            lagged(pool, HC, 3, body2, first=4)

            def masks3(jj, b, quarters):
                for n in quarters:
                    i, k = divmod(n, NQ)
                    pool.wait_ge(rows3_in[k % 2], 16 * (HT * NQ // 2 * jj + n // 2 + 1))
                    wait(pool, sc3_out, NQ * (STEPS * (jj - 1) - HT + i) + k + 1)
                    apart(pool, passed_pool)
                    pool.tensor_scalar(masks[b][i][:, k * QW:(k + 1) * QW], rows3[k % 2][:, :], 0.0, MASKED,
                                       ALU.is_equal, ALU.mult).then_inc(mask_done, 1)

            def residual3(jj):
                pool.wait_ge(att_done, HEADS * HT * (jj + 1))
                pool.wait_ge(rest_loaded, 16 * (jj + 1))
                wait(pool, fin3, FIN3 * jj)
                pool.tensor_tensor(diff[:, :], skip_in, att[:, :], ALU.subtract).then_inc(diff_pool, 1)
                pool.tensor_tensor(base[:, :], att[:, :], x3_in, ALU.add).then_inc(diff_pool, 1)

            def finish3(jj):
                pool.wait_ge(fin3, FIN3 * (jj + 1))
                inverse_root(rstd[:, 0:HT], var_e[:, 0:HT], mv[:, 0:HT, 1], EPS, ALU.add, HT, rstd_pool[3], 4 * jj)
                pool.wait_ge(rstd_pool[3], 4 * jj + 2)
                wait(pool, stored, 16 * jj)
                apart(pool, passed_pool)
                for i in range(HT):
                    pool.tensor_scalar(out3[:, i * P:(i + 1) * P], res3[:, i * P:(i + 1) * P], mv[:, i, 0:1],
                                       rstd[:, i:i + 1], ALU.subtract, ALU.mult).then_inc(rstd_pool[3], 1)
                pool.wait_ge(rstd_pool[3], 4 * jj + 4)
                dst = out_v[bass.ds(jj, 1), :, :, :].rearrange("o p i d -> (o p) i d")
                pool.dma_start(dst, out3[:, :].rearrange("p (i d) -> p i d", i=HT)).then_inc(stored, 16)

            def step3(jj, b):
                last = isinstance(jj, int) and jj >= HC - 1
                first = isinstance(jj, int) and jj == 0
                if not last:
                    masks3(jj + 1, 1 - b, range(0, 3))
                if not first:
                    residual3(jj - 1)
                if not last:
                    masks3(jj + 1, 1 - b, range(3, 6))
                if not first:
                    finish3(jj - 1)
                if not last:
                    masks3(jj + 1, 1 - b, range(6, HT * NQ))

            pool.wait_ge(mix_done, 2 * UNITS * HC)
            masks3(0, 0, range(HT * NQ))
            pool.wait_ge(x3c_done, NC)
            pool.wait_ge(x3_saved, 16)
            step3(0, 0)
            with pool.Fori(0, (HC - 2) // 2) as t:
                step3(2 * t + 1, 1)
                step3(2 * t + 2, 0)
            step3(HC - 1, 1)
            step3(HC, 0)
            pool.wait_ge(stored, 16 * HC)

        @block.vector
        def _(dve):
            dve.wait_ge(alpha0_in, 16)
            dve.tensor_scalar(keep0, alpha0, -1.0, 1.0, ALU.mult, ALU.add).then_inc(setup_dve, 1)

            def setup():
                dve.wait_ge(late_in, 16 * N_LATE)
                dve.tensor_tensor(gate_out[:, :], gate_w[:, 0:D], gate_w[:, 2 * D:3 * D], ALU.add).then_inc(setup_dve, 1)
                dve.tensor_tensor(gate_skip[:, :], gate_w[:, D:2 * D], gate_w[:, 2 * D:3 * D], ALU.subtract).then_inc(setup_dve, 1)
                dve.wait_ge(setup_act, 1)
                dve.tensor_scalar(sig_d, sig_e, 1.0, None, ALU.add).then_inc(setup_dve, 1)
                dve.wait_ge(setup_dve, 4)
                dve.reciprocal(sig2, sig_d).then_inc(setup_dve, 1)
                dve.wait_ge(setup_dve, 5)
                dve.tensor_scalar(negsig2, sig2, -1.0, None, ALU.mult).then_inc(setup_dve, 1)
                dve.wait_ge(setup_dve, 6)

            def quarter2(jj, b, u):
                i, k = divmod(u, NQ)
                tau = UNITS * jj + u
                dve.wait_ge(sc2_mm, tau + 1)
                if k == 0:
                    dve.wait_ge(rows2_in[i], 16 * (jj + 1))
                wait(dve, turn2, 2 * UNITS * (jj - 2) + 4 * k + 4)
                apart(dve, passed_dve)
                m = slice(k * QW, (k + 1) * QW)
                dve.tensor_tensor_reduce(prob[b][i][:, m], pair[k % 2][:, :], rows2[i][:, m], beta2, -3.0e38,
                                         ALU.mult, ALU.max, qmax2[:, i, k:k + 1]).then_inc(sc2_out, 1)
                if k == NQ - 1:
                    dve.wait_ge(sc2_out, tau + 1)
                    dve.tensor_reduce(negmax2[:, i:i + 1], qmax2[:, i, :], AX.X, ALU.max, negate=True)\
                        .then_inc(max2, 1)

            for l in range(2):
                x_res, x_out = (xa, xb) if l == 0 else (xb, xa)
                chain = Chain(dve, lin_chain[l], CHAIN01[l])

                def body(j, b, l=l, x_res=x_res, x_out=x_out, chain=chain):
                    def row_sums(groups):
                        if l == 0 and inside(j, NC):
                            for g in groups:
                                if g == 0:
                                    wait(dve, lin_mm[0], j - 1)
                                dve.wait_ge(cols_in[g], 16 * (j + 1))
                                dve.tensor_reduce(part[b][:, g, :].rearrange("p (h n) -> p h n", h=2),
                                                  cols[g][:, :, :, :].rearrange("p h m n -> p h n m"),
                                                  AX.X, ALU.add).then_inc(part_done, 1)

                    row_sums(range(2))
                    if inside(j - 1, NC):
                        o = 1 - b
                        chain.round(j - 1)
                        dve.wait_ge(lin_mm[l], j)
                        if l == 0:
                            chain.add(dve.tensor_copy(rowsum[:, bass.ds(CT * (j - 1), CT)], sums[:, 0:CT]))
                            chain.link(dve.tensor_scalar(deg, sums[:, 0:CT], alpha0, keep0, ALU.mult, ALU.add))
                            chain.add(dve.scalar_tensor_tensor(deg_safe, deg, 0.0, deg, ALU.is_equal, ALU.add))
                            chain.link(dve.tensor_scalar(deg_nz, deg, 0.0, None, ALU.not_equal))
                            chain.link(dve.reciprocal(deg_inv, deg_safe))
                            chain.link(dve.tensor_tensor(inv, deg_inv, deg_nz, ALU.mult))
                            for i in range(CT):
                                chain.add(dve.scalar_tensor_tensor(
                                    lin[:, i * P:(i + 1) * P], turned[o][:, i * P:(i + 1) * P], inv[:, i:i + 1],
                                    bias0[:, :], ALU.mult, ALU.add))
                        else:
                            for i in range(CT):
                                chain.add(dve.tensor_tensor(lin[:, i * P:(i + 1) * P], turned[o][:, i * P:(i + 1) * P],
                                                            bias1[:, :], ALU.add))
                        chain.sync()
                        chain.link(dve.scalar_tensor_tensor(res[:, :], lin[:, :], 0.0,
                                                            x_res[:, bass.ds(CW * (j - 1), CW)], ALU.max, ALU.add))
                        for i in range(CT):
                            chain.add(dve.bn_stats(stats[:, i, :], res[:, i * P:(i + 1) * P]))
                        chain.sync()
                        apart(dve, passed_dve)
                        for i in range(CT):
                            chain.add(dve.bn_aggr(mv[:, i, :], stats[:, i, :]))
                        last = l == 1 and isinstance(j, int) and j == NC
                        if last:
                            quarter2(0, 0, 0)
                        dve.wait_ge(rstd_pool[l], 2 * j)
                        chain.sync()
                        for i in range(CT):
                            chain.add(dve.tensor_scalar(
                                x_out[:, bass.ds(CW * (j - 1) + i * P, P)], res[:, i * P:(i + 1) * P],
                                mv[:, i, 0:1], rstd[:, i:i + 1], ALU.subtract, ALU.mult))
                        chain.done()
                        if l == 1:
                            chain.sync()
                            if last:
                                for u in range(1, EARLY2):
                                    quarter2(0, 0, u)
                            dve.wait_ge(rn_pool, 2 * j)
                            wait(dve, xn_turn, j - 1)
                            for i in range(CT):
                                dve.tensor_scalar(xn[:, i * P:(i + 1) * P], xa[:, bass.ds(CW * (j - 1) + i * P, P)],
                                                  ssq[:, 2, i:i + 1], None, ALU.mult).then_inc(xn_done, 1)
                    row_sums(range(2, GROUPS))
                    if isinstance(j, int) and j == 0:
                        if l == 0:
                            dve.wait_ge(setup_dve, 1)
                            dve.wait_ge(early_in, 16 * N_EARLY)
                            for g in range(GROUPS):
                                dve.wait_ge(x_loaded[g], 16)
                        else:
                            setup()
                    if l == 0 and inside(j, NC):
                        dve.wait_ge(keep_ready, j + 1)
                        dve.wait_ge(agg_mm[0], GROUPS * (j + 1))
                        dve.scalar_tensor_tensor(agg[b][:, :], pair[b][:, 0:CW], alpha0,
                                                 keep_xt[:, bass.ds(CW * j, CW)], ALU.mult, ALU.add)\
                            .then_inc(agg_out[0], 1)
                    if l == 1 and inside(j - 1, NC):
                        dve.wait_ge(hi_done, j)
                        m = bass.ds(CW * (j - 1), CW)
                        dve.tensor_tensor(xn_lo[:, m], turned[2][:, :], xn_hi[:, m].bitcast(F32), ALU.subtract)\
                            .then_inc(lo_done, 1)

                lagged(dve, NC, 1, body)

            dve.wait_ge(dis_done, 2)
            dve.wait_ge(lo_done, NC)
            fin = Chain(dve, fin2, FIN2)

            def mix_tiles(r, slot, v, s, c):
                dve.wait_ge(turn2, r + 1)
                dve.wait_ge(cols2_in[v % 4], 16 * (UNITS // 4 * c + v // 4 + 1))
                wait(dve, mix_mm, r - 3)
                for m in range(2):
                    t = 4 * v + 2 * s + m
                    ins = dve.scalar_tensor_tensor(mix[(2 * v + s) % 4][:, m, :], cols2[v % 4][:, 2 * s + m, :],
                                                   dis[:, t:t + 1], turned[slot][:, m * HW:(m + 1) * HW],
                                                   ALU.mult, ALU.add)
                ins.then_inc(mix_done, 1)

            def norm2(jj, i):
                n = HT * jj + i
                dve.wait_ge(exp2, n + 1)
                dve.tensor_tensor(nrm2[:, 0, i:i + 1], den2[:, i:i + 1], dis[:, bass.ds(n, 1)], ALU.mult).then_inc(nrm_chain, 1)
                dve.wait_ge(nrm_chain, 3 * n + 1)
                dve.reciprocal(nrm2[:, 1, i:i + 1], nrm2[:, 0, i:i + 1]).then_inc(nrm_chain, 1)
                dve.wait_ge(nrm_chain, 3 * n + 2)
                dve.tensor_tensor(nrm2[:, 2, i:i + 1], nrm2[:, 1, i:i + 1], sig2, ALU.mult).then_inc(nrm_chain, 1)

            def body2(jj, b):
                for u in range(UNITS):
                    i, k = divmod(u, NQ)
                    tau = UNITS * jj + u
                    v = (u - LAG2) % UNITS
                    c = jj + (u - LAG2) // UNITS
                    r = 2 * (tau - LAG2)
                    if inside(c, HC):
                        mix_tiles(r, 0, v, 0, c)
                    if u == 1 and inside(jj - 1, HC):
                        norm2(jj - 1, 1)
                    if u == 5 and inside(jj, HC):
                        norm2(jj, 0)
                    if inside(jj, HC) and not (isinstance(jj, int) and tau < EARLY2):
                        quarter2(jj, b, u)
                    if inside(c, HC):
                        mix_tiles(r + 1, 1, v, 1, c)
                    if u == 6 and inside(jj - 2, HC):
                        fin.round(jj - 2)
                        dve.wait_ge(nat2, jj - 1)
                        for i2 in range(HT):
                            fin.add(dve.tensor_scalar(lin2[:, i2 * P:(i2 + 1) * P], mix_sums[b][:, i2 * P:(i2 + 1) * P],
                                                      dis[:, bass.ds(HT * (jj - 2) + i2, 1)], None, ALU.mult))
                        fin.sync()
                        fin.link(dve.scalar_tensor_tensor(res2[:, :], xa[:, bass.ds(HW * (jj - 2), HW)], negsig2,
                                                          lin2[:, :], ALU.mult, ALU.add))
                        for i2 in range(HT):
                            fin.add(dve.bn_stats(stats[:, i2, :], res2[:, i2 * P:(i2 + 1) * P]))
                        fin.sync()
                        apart(dve, passed_dve)
                        for i2 in range(HT):
                            fin.add(dve.bn_aggr(mv[:, i2, :], stats[:, i2, :]))
                        fin.done()
                    if u == 7 and inside(jj - 2, HC):
                        dve.wait_ge(fin2, FIN2 * (jj - 1))
                        dve.wait_ge(rstd_pool[2], 2 * (jj - 1))
                        for i2 in range(HT):
                            ins = dve.tensor_scalar(xb[:, bass.ds(HW * (jj - 2) + i2 * P, P)],
                                                    res2[:, i2 * P:(i2 + 1) * P], mv[:, i2, 0:1], rstd[:, i2:i2 + 1],
                                                    ALU.subtract, ALU.mult)
                        ins.then_inc(x3_done, 1)

            lagged(dve, HC, 2, body2)

            dve.wait_ge(x3_done, HC)

            def project(j, b):
                def plus(n, o, bias, dst):
                    dve.wait_ge(pp_mm, PPM * j + n)
                    dve.tensor_tensor(dst.rearrange("p (i d) -> p i d", d=D), o[:, :].rearrange("p (i d) -> p i d", d=D),
                                      bias[:, :].rearrange("p (o d) -> p o d", o=1).broadcast_to([P, CT, D]), ALU.add)\
                        .then_inc(pp_dve, 1)

                def low(n, o, bias, dst):
                    dve.wait_ge(pp_act, PPA * j + n)
                    dve.scalar_tensor_tensor(dst[:, 1, :], o[:, :], bias[:, :], dst[:, 0, :].bitcast(F32),
                                             ALU.add, ALU.subtract).then_inc(pp_dve, 1)

                plus(1, turned[0], bias_v, xa[:, bass.ds(CW * j, CW)])
                low(1, turned[2], bk, k_out[b])
                wait(dve, skip_saved[b], 16 * (j - b))
                plus(3, turned[1], bias_s, skip_out[b][:, :])
                low(2, turned[0], bq, q_out[b])
                for h in range(2, HEADS):
                    dve.wait_ge(pp_mm, PPM * j + 5 + h)
                    dve.tensor_copy(keys[h][:, bass.ds(CW * j, CW)], banks[h]).then_inc(pp_dve, 1)

            lagged(dve, NC, 0, project)

            dve.memset(qmax3[:, :, NQ:NQ + 1], FLOOR).then_inc(floor_set, 1)
            dve.wait_ge(floor_set, 1)
            fin = Chain(dve, fin3, FIN3)
            att_v = att[:, :].rearrange("p (i c h) -> p i c h", i=HT, h=HEADS)

            def masked(jj, b, s, k):
                h, i = divmod(s, HT)
                sg = STEPS * jj + s
                dve.wait_ge(sc3_mm, NQ * sg + k + 1)
                if h == 0:
                    dve.wait_ge(mask_done, HT * NQ * jj + NQ * i + k + 1)
                if not (isinstance(jj, int) and STEPS * jj + s < 2):
                    at = counts(jj, (s - 2,), (2 * k, 2 * k + 1))
                    if "act" in at:
                        dve.wait_ge(turn_a, at["act"])
                    if "dve" in at:
                        dve.wait_ge(turn_d, at["dve"])
                apart(dve, passed_dve)
                m = slice(k * QW, (k + 1) * QW)
                dve.tensor_tensor_reduce(score[s % 2][:, m], pair[k % 2][:, :], masks[b][i][:, m], float(C) ** -0.5, -3.0e38,
                                         ALU.add, ALU.max, qmax3[:, s % 2, k:k + 1]).then_inc(sc3_out, 1)

            def out_of_psum(jj, s, q):
                if (s % STEPS, q) in take and take[s % STEPS, q][0] == "dve":
                    _, n = order(jj, s, q)
                    i = s % HT
                    dve.wait_ge(turn_d, n + 1)
                    dve.tensor_copy(probt[:, 4 * q:4 * q + 4, i * P:(i + 1) * P],
                                    turned[2][:, :].rearrange("p (m n) -> p m n", m=4)).then_inc(ev_d, 1)

            def step3(jj, b, s):
                h, i = divmod(s, HT)
                live = tile(jj, s)

                def out(lag, q):
                    if isinstance(jj, int) and (jj, s, lag) == (0, 1, 1):
                        projections_over(dve)
                    if tile(jj, s - lag):
                        out_of_psum(jj, s - lag, q)

                group = i == 0 and tile(jj, HT * (h - 2))
                gg, hd = HEADS * jj + h - 2, (h - 2) % HEADS
                if live:
                    masked(jj, b, s, 0)
                out(2, 5)
                if group:
                    dve.wait_ge(exp3, 2 * HT * (gg + 1))
                    dve.scalar_tensor_tensor(dsum[:, hd, :], den3[:, hd, 0, :], 1e-30, den3[:, hd, 1, :],
                                             ALU.max, ALU.add).then_inc(dinv_chain, 1)
                if live:
                    masked(jj, b, s, 1)
                if group:
                    dve.wait_ge(dinv_chain, 2 * gg + 1)
                    dve.reciprocal(dinv[:, hd, :], dsum[:, hd, :]).then_inc(dinv_chain, 1)
                out(2, 7)
                if live:
                    masked(jj, b, s, 2)
                out(1, 2)
                if group:
                    dve.wait_ge(head_nat, gg + 1)
                    dve.wait_ge(dinv_chain, 2 * (gg + 1))
                    if hd == 0:
                        wait(dve, diff_pool, 2 * jj)
                    for i2 in range(HT):
                        dve.tensor_scalar(att_v[:, i2, :, hd], sums[:, C * i2:C * i2 + C],
                                          dinv[:, hd, i2:i2 + 1], None, ALU.mult).then_inc(att_done, 1)
                if live:
                    masked(jj, b, s, 3)
                    dve.wait_ge(sc3_out, NQ * (STEPS * jj + s + 1))
                    dve.tensor_reduce(negmax3[:, s % 2:s % 2 + 1], qmax3[:, s % 2, :], AX.X, ALU.max, negate=True)\
                        .then_inc(max3, 1)
                if s == 3 and tile(jj, -1):
                    dve.wait_ge(att_done, HEADS * HT * jj)
                    dve.wait_ge(rest_loaded, 16 * jj)
                    for i2 in range(HT):
                        m = slice(i2 * D, (i2 + 1) * D)
                        dve.tensor_tensor_reduce(dot_o[:, :], att[:, m], gate_out[:, :], 1.0, 0.0,
                                                 ALU.mult, ALU.add, dots[:, 0, i2:i2 + 1]).then_inc(dots_done, 1)
                        dve.wait_ge(dots_done, 4 * (jj - 1) + 2 * i2 + 1)
                        dve.tensor_tensor_reduce(dot_o[:, :], rest_in[:, 0, m], gate_skip[:, :], 1.0, dots[:, 0, i2:i2 + 1],
                                                 ALU.mult, ALU.add, dots[:, 1, i2:i2 + 1]).then_inc(dots_done, 1)
                        dve.wait_ge(dots_done, 4 * (jj - 1) + 2 * i2 + 2)
                if s == 5 and tile(jj, -1):
                    fin.round(jj - 1)
                    dve.wait_ge(gate_act, jj)
                    fin.link(dve.tensor_scalar(dots[:, 3, :], dots[:, 2, :], 1.0, None, ALU.add))
                    fin.link(dve.reciprocal(dots[:, 4, :], dots[:, 3, :]))
                    dve.wait_ge(diff_pool, 2 * jj)
                    wait(dve, rstd_pool[3], 4 * (jj - 1))
                    for i2 in range(HT):
                        m = slice(i2 * D, (i2 + 1) * D)
                        fin.add(dve.scalar_tensor_tensor(res3[:, m], diff[:, m], dots[:, 4, i2:i2 + 1], base[:, m],
                                                         ALU.mult, ALU.add))
                    fin.sync()
                    for i2 in range(HT):
                        fin.add(dve.bn_stats(stats[:, i2, :], res3[:, i2 * P:(i2 + 1) * P]))
                    fin.sync()
                    apart(dve, passed_dve)
                    for i2 in range(HT):
                        fin.add(dve.bn_aggr(mv[:, i2, :], stats[:, i2, :]))
                    fin.done()

            for jj in range(2):
                for s in range(STEPS):
                    step3(jj, jj, s)
            with dve.Fori(1, HC // 2) as t:
                for b in range(2):
                    for s in range(STEPS):
                        step3(2 * t + b, b, s)
            for s in (0, 1, 2, 3, 5):
                step3(HC, 0, s)

    return nc


_OUT = (N, D)


def kernel(**inputs):
    import numpy as np
    import concourse.bacc as bacc
    from concourse.bass_utils import run_bass_kernel_spmd

    f = {k: np.asarray(v) for k, v in inputs.items()}
    adj = f["adj"]
    arrays = {
        "adj_rows": adj,
        "adj_cols": adj.reshape(HC, HW, NT, P).transpose(0, 3, 2, 1),
        "x": f["x"],
        "x_t": f["x"].T,
        "w0_t": f["L0_gnn_W"].T,
        "w1": f["L1_gnn_kernel"],
        "wv": f["L3_gnn_Wv"], "ws": f["L3_gnn_Ws"], "wq": f["L3_gnn_Wq"], "wk": f["L3_gnn_Wk"],
        "b0": f["L0_gnn_b"], "b1": f["L1_gnn_bias"], "bv": f["L3_gnn_bv"], "bs": f["L3_gnn_bs"],
        "bq": f["L3_gnn_bq"].reshape(P, 1), "bk": f["L3_gnn_bk"].reshape(P, 1),
        "wb": f["L3_gnn_Wb"].reshape(3 * D),
        "alpha0": f["L0_gnn_alpha"].reshape(1),
        "alpha2": f["L2_gnn_alpha"].reshape(1),
        "beta2": f["L2_gnn_beta"].reshape(1),
        "ident": np.eye(P, dtype=np.float32),
        "spread": np.einsum("gh,cd,wb->gchwbd", np.eye(HEADS), np.eye(C), np.repeat(np.eye(2), 2, axis=1))
                    .reshape(P, HEADS, 2, P).astype(np.float32),
        "stack": np.tile(np.eye(C, dtype=np.float32), (4, 1)),
    }
    arrays = {k: np.ascontiguousarray(v) for k, v in arrays.items()}
    nc = bacc.Bacc("TRN2", target_bir_lowering=False, num_devices=1)
    args = {k: nc.dram_tensor(f"in_{k}", v.shape, mybir.dt.from_np(v.dtype), kind="ExternalInput").ap()
            for k, v in arrays.items()}
    args["out"] = nc.dram_tensor("out_x", _OUT, F32, kind="ExternalOutput").ap()
    graph_layers(nc, args)
    r = run_bass_kernel_spmd(nc, [{f"in_{k}": v for k, v in arrays.items()}], core_ids=[0])
    return r.results[0]["out_x"]
```
